# Optimizing a Trainium2 kernel written in Bass

```python
import numpy as np
import jax
import jax.numpy as jnp

def _softmax(x, axis=-1):
    return jax.nn.softmax(x, axis=axis)

def _gelu(x):
    return jax.nn.gelu(x, approximate=True)

def _silu(x):
    return jax.nn.silu(x)

def _sigmoid(x):
    return jax.nn.sigmoid(x)

def _layernorm(x, axis=-1, eps=1e-05):
    m = jnp.mean(x, axis=axis, keepdims=True)
    v = jnp.var(x, axis=axis, keepdims=True)
    return (x - m) / jnp.sqrt(v + eps)

def _scatter_add(tgt, idx, src, axis=0):
    return tgt.at[idx].add(src)

def _segment_sum(src, seg, n):
    return jax.ops.segment_sum(src, seg, n)
kernel_name = 'mk_xattn_ffn_d1_seqx_r8_7311ae'

def setup_inputs(seed: int=0):
    np.random.seed(seed)
    _w = jnp.asarray

    def _rec_inputs():
        import jax
        import jax.numpy as jnp
        _rk = jax.random.key(seed)
        x = -0.0002928 + 1 * jax.random.normal(jax.random.fold_in(_rk, 1), (4, 256, 128), jnp.float32)
        _lenS = 256 - jax.random.randint(jax.random.fold_in(_rk, 7), (4,), 0, max(1, 256 // 4) + 1, jnp.int32)
        _lenS2 = 512 - jax.random.randint(jax.random.fold_in(_rk, 8), (4,), 0, max(1, 512 // 4) + 1, jnp.int32)
        _ctx_1024P = jax.random.normal(jax.random.fold_in(_rk, 11), (4, 16, 128), jnp.float32)
        _ctx_1024c = jax.random.dirichlet(jax.random.fold_in(_rk, 511), 0.3 * jnp.ones((16,), jnp.float32), (4, 512))
        _ctx_1024t = jnp.einsum('bsk,bkd->bsd', _ctx_1024c, _ctx_1024P)
        _ctx_1024t = _ctx_1024t * jax.lax.rsqrt(jnp.mean(jnp.square(_ctx_1024t)) + 1e-12) * 0.953939
        ctx_1024 = -1.39393e-06 + 0.999914 * (_ctx_1024t + 0.3 * jax.random.normal(jax.random.fold_in(_rk, 611), (4, 512, 128), jnp.float32))
        _validS = jnp.arange(256)[None, :] < _lenS[:, None]
        _validS2 = jnp.arange(512)[None, :] < _lenS2[:, None]
        _causal = jnp.tril(jnp.ones((256, 256), dtype=bool))
        mask_1xSxS2_bk1 = jnp.broadcast_to(_validS2[0:1, None, :], (1, 256, 512))
        return (x, ctx_1024, mask_1xSxS2_bk1)
    x, ctx_1024, mask_1xSxS2_bk1 = _rec_inputs()

    def _L0_xattn_setup():
        import jax, jax.numpy as jnp
        import numpy as np
        B, S, D = (2, 256, 128)
        H, DH = (16, 64)

        def _split_heads(x):
            b, s, _ = x.shape
            return x.reshape(b, s, H, DH).transpose(0, 2, 1, 3)
        key = jax.random.key(seed)
        ks = jax.random.split(key, 12)
        scale = 1.0 / np.sqrt(D)
        inp = {'queries': jax.random.normal(ks[0], (B, S, D), jnp.float32), 'keys': jax.random.normal(ks[1], (B, S, D), jnp.float32), 'values': jax.random.normal(ks[2], (B, S, D), jnp.float32), 'mask': jnp.triu(jnp.ones((1, S, S), dtype=bool), k=1), 'Wq': jax.random.normal(ks[3], (D, H * DH), jnp.float32) * scale, 'bq': jnp.zeros((H * DH,), jnp.float32), 'Wk': jax.random.normal(ks[4], (D, H * DH), jnp.float32) * scale, 'bk': jnp.zeros((H * DH,), jnp.float32), 'Wv': jax.random.normal(ks[5], (D, H * DH), jnp.float32) * scale, 'bv': jnp.zeros((H * DH,), jnp.float32), 'Wo': jax.random.normal(ks[6], (H * DH, D), jnp.float32) * scale, 'bo': jnp.zeros((D,), jnp.float32)}
        return inp
    _L0_xattn_all = _L0_xattn_setup()
    _L0_xattn_in = {k: v for k, v in _L0_xattn_all.items() if k in ('Wq', 'bq', 'Wk', 'bk', 'Wv', 'bv', 'Wo', 'bo')}
    del _L0_xattn_all

    def _L0_ffn_setup():
        import jax, jax.numpy as jnp
        import numpy as np
        D_MODEL = 128
        MLP_DIM = 512
        N_EXPERTS = 8
        B, T = (4, 128)
        key = jax.random.key(seed)
        ks = jax.random.split(key, 7)
        scale_in = (1.0 / D_MODEL) ** 0.5
        scale_out = (1.0 / MLP_DIM) ** 0.5
        bound_g = (1.0 / D_MODEL) ** 0.5
        w_gate = jax.random.uniform(ks[0], (D_MODEL, N_EXPERTS), minval=-bound_g, maxval=bound_g, dtype=jnp.float32)
        b_gate = jax.random.uniform(ks[1], (N_EXPERTS,), minval=-bound_g, maxval=bound_g, dtype=jnp.float32)
        W1 = jax.random.uniform(ks[2], (N_EXPERTS, D_MODEL, MLP_DIM), minval=-scale_in, maxval=scale_in, dtype=jnp.float32)
        b1 = jnp.zeros((N_EXPERTS, MLP_DIM), dtype=jnp.float32)
        W2 = jax.random.uniform(ks[3], (N_EXPERTS, MLP_DIM, D_MODEL), minval=-scale_out, maxval=scale_out, dtype=jnp.float32)
        b2 = jnp.zeros((N_EXPERTS, D_MODEL), dtype=jnp.float32)
        x = jax.random.normal(ks[4], (B, T, D_MODEL), dtype=jnp.float32)
        return {'x': x, 'w_gate': w_gate, 'b_gate': b_gate, 'W1': W1, 'b1': b1, 'W2': W2, 'b2': b2}
    _L0_ffn_all = _L0_ffn_setup()
    _L0_ffn_in = {k: v for k, v in _L0_ffn_all.items() if k in ('w_gate', 'b_gate', 'W1', 'b1', 'W2', 'b2')}
    del _L0_ffn_all
    return {'x': x, 'ctx_1024': ctx_1024, 'mask_1xSxS2_bk1': mask_1xSxS2_bk1, 'L0_xattn_Wq': _L0_xattn_in['Wq'], 'L0_xattn_bq': _L0_xattn_in['bq'], 'L0_xattn_Wk': _L0_xattn_in['Wk'], 'L0_xattn_bk': _L0_xattn_in['bk'], 'L0_xattn_Wv': _L0_xattn_in['Wv'], 'L0_xattn_bv': _L0_xattn_in['bv'], 'L0_xattn_Wo': _L0_xattn_in['Wo'], 'L0_xattn_bo': _L0_xattn_in['bo'], 'L0_ffn_w_gate': _L0_ffn_in['w_gate'], 'L0_ffn_b_gate': _L0_ffn_in['b_gate'], 'L0_ffn_W1': _L0_ffn_in['W1'], 'L0_ffn_b1': _L0_ffn_in['b1'], 'L0_ffn_W2': _L0_ffn_in['W2'], 'L0_ffn_b2': _L0_ffn_in['b2']}

def reference(x, ctx_1024, mask_1xSxS2_bk1, L0_xattn_Wq, L0_xattn_bq, L0_xattn_Wk, L0_xattn_bk, L0_xattn_Wv, L0_xattn_bv, L0_xattn_Wo, L0_xattn_bo, L0_ffn_w_gate, L0_ffn_b_gate, L0_ffn_W1, L0_ffn_b1, L0_ffn_W2, L0_ffn_b2):
    import jax
    import jax.numpy as jnp

    def _L0_xattn_ref(queries, keys, values, mask, Wq, bq, Wk, bk, Wv, bv, Wo, bo):
        import jax, jax.numpy as jnp
        import numpy as np
        B, S, D = (2, 256, 128)
        H, DH = (16, 64)

        def _split_heads(x):
            b, s, _ = x.shape
            return x.reshape(b, s, H, DH).transpose(0, 2, 1, 3)
        q = _split_heads(queries @ Wq + bq)
        k = _split_heads(keys @ Wk + bk)
        v = _split_heads(values @ Wv + bv)
        scores = jnp.einsum('bhqd,bhkd->bhqk', q, k) / jnp.sqrt(jnp.float32(DH))
        m = mask[:, None, :, :]
        scores = jnp.where(m, -jnp.inf, scores)
        attn = jax.nn.softmax(scores, axis=-1)
        ctx = jnp.einsum('bhqk,bhkd->bhqd', attn, v)
        ctx = ctx.transpose(0, 2, 1, 3).reshape(queries.shape[0], S, H * DH)
        return ctx @ Wo + bo

    def _L0_ffn_ref(x, w_gate, b_gate, W1, b1, W2, b2):
        import jax, jax.numpy as jnp
        import numpy as np
        D_MODEL = 128
        MLP_DIM = 512
        N_EXPERTS = 8
        B, T = (4, 128)
        b, t, d = x.shape
        x_flat = x.reshape(b * t, d)
        logits = x_flat @ w_gate + b_gate
        probs = jax.nn.softmax(logits, axis=-1)
        route_p = jnp.max(probs, axis=-1)
        route_idx = jnp.argmax(probs, axis=-1)
        h = jnp.einsum('nd,edm->enm', x_flat, W1) + b1[:, None, :]
        h = jax.nn.relu(h)
        y = jnp.einsum('enm,emd->end', h, W2) + b2[:, None, :]
        n = b * t
        out = y[route_idx, jnp.arange(n)] * route_p[:, None]
        return out.reshape(b, t, d)
    x = x + _L0_xattn_ref(_layernorm(x, axis=-1), ctx_1024, ctx_1024, mask_1xSxS2_bk1, L0_xattn_Wq, L0_xattn_bq, L0_xattn_Wk, L0_xattn_bk, L0_xattn_Wv, L0_xattn_bv, L0_xattn_Wo, L0_xattn_bo)
    x = x + _L0_ffn_ref(_layernorm(x, axis=-1), L0_ffn_w_gate, L0_ffn_b_gate, L0_ffn_W1, L0_ffn_b1, L0_ffn_W2, L0_ffn_b2)
    return x

_drawn_inputs = setup_inputs


def setup_inputs(seed=0):
    import zlib

    import numpy as np

    out = dict(_drawn_inputs(seed))
    spreads = {'L0_xattn_bq': (0.0, 0.1),
     'L0_xattn_bk': (0.0, 0.8),
     'L0_xattn_bv': (0.0, 0.1),
     'L0_xattn_bo': (0.0, 0.1),
     'L0_ffn_b1': (0.0, 0.8),
     'L0_ffn_b2': (0.0, 0.573)}
    factors = {'L0_ffn_b_gate': 6.857}
    for name, (base, spread) in spreads.items():
        noise = np.random.default_rng([zlib.crc32(name.encode()), seed]).standard_normal(out[name].shape)
        drawn = base * np.exp(spread * noise) if base else spread * noise
        out[name] = jnp.asarray(drawn.astype(out[name].dtype))
    for name, factor in factors.items():
        out[name] = (out[name] * factor).astype(out[name].dtype)
    return out
```

```python
from contextlib import ExitStack

import concourse.bass as bass
from concourse import mybir
from concourse.alu_op_type import AluOpType as ALU

ACT = mybir.ActivationFunctionType
AX = mybir.AxisListType
F32 = mybir.dt.float32
BF16 = mybir.dt.bfloat16
I32 = mybir.dt.int32
U8 = mybir.dt.uint8

P = 128
BANK = 512
TAIL = 64
MASKED = -1e30
HUGE = 3e38
EPS = 1e-5


def xattn_moe(nc, x, ctx_in, mask, Wq, bq, Wk, bk, Wv, bv, Wo, bo,
              w_gate, b_gate, W1, b1, W2, b2, out):
    B, S, D = x.shape
    SK = ctx_in.shape[1]
    HD = Wq.shape[1]
    DH = 64
    H = HD // DH
    E = w_gate.shape[1]
    F = W1.shape[2]
    QT = S // P
    NT = B * QT
    FT = HD // P
    HC = F // P
    SCALE = DH ** -0.5
    assert D == P and FT * 2 == H and QT == 2 and S % P == 0 and SK % P == 0

    with ExitStack() as stack:
        def sb(name, shape, dt=F32):
            return stack.enter_context(nc.sbuf_tensor(name, shape, dt))

        def sem(name):
            return stack.enter_context(nc.semaphore(name))

        banks = [stack.enter_context(nc.psum_tensor(f"bank{i}", [P, BANK], F32)) for i in range(8)]
        score_bank = [[banks[0], banks[1]], [banks[2], banks[3]]]
        ring_bank = banks[4:7]
        out_bank = banks[7]

        x_tok = sb("x_tok", [P, B, QT, D])
        mask_u8 = sb("mask_u8", [P, QT, SK], U8)
        ctx_tail = sb("ctx_tail", [P, 2, D])
        ctx_all = sb("ctx_all", [P, SK // P, D])
        wq_sb = sb("wq_sb", [P, HD])
        wk_sb = sb("wk_sb", [P, HD])
        wv_sb = sb("wv_sb", [P, HD])
        wo_sb = sb("wo_sb", [P, FT, D])
        bo_row = sb("bo_row", [1, D])
        NB = 3 * FT + E * HC
        bias_rows = sb("bias_rows", [NB, P])
        wg_sb = sb("wg_sb", [P, E])
        bg_row = sb("bg_row", [1, E])
        w1_sb = sb("w1_sb", [P, E, F])
        w2_sb = sb("w2_sb", [P, E, HC, D])
        b2_sb = sb("b2_sb", [E, D])

        ident = sb("ident", [P, P])
        ident_bf = sb("ident_bf", [P, P], BF16)
        ones = sb("ones", [P, P])
        minus_half = sb("minus_half", [P, NT])
        iota8 = sb("iota8", [P, NT, E])

        stats = sb("stats", [P, NT, nc.vector.BN_STATS_DIM])
        mean_var = sb("mean_var", [P, NT, nc.vector.BN_AGGR_DIM])
        var_eps = sb("var_eps", [P, NT])
        rstd = sb("rstd", [P, NT])
        normed = sb("normed", [P, NT, D])
        normed_T = sb("normed_T", [P, NT * P])
        bias_T = sb("bias_T", [P, NB])
        bq_scaled = sb("bq_scaled", [P, FT])
        row_min = sb("row_min", [P, QT])
        far_min = sb("far_min", [P, 1])
        blown = sb("blown", [P, QT])
        dead_row = sb("dead_row", [P, QT])
        short_flag = sb("short_flag", [1, 1], I32)

        mask_bias = sb("mask_bias", [P, QT, BANK], BF16)
        ctx_T = sb("ctx_T", [P, BANK])
        q_T = sb("q_T", [P, 2, FT, S])
        k_T = sb("k_T", [P, FT, BANK])
        v_T = sb("v_T", [P, FT, BANK])
        VO_BLOCKS = H * SK // P
        vo = sb("vo", [P, VO_BLOCKS, D])
        neg_max = sb("neg_max", [P, 2, 2, 8])
        row_sum = sb("row_sum", [P, 2, 2, 8])
        inv_sum = sb("inv_sum", [P, 2, 2, 8])
        probs = sb("probs", [P, 2, 2, BANK])
        probs_T = sb("probs_T", [P, 2, BANK])
        x1 = sb("x1", [P, NT, D])

        gate_e = sb("gate_e", [P, NT, E])
        gate_a = sb("gate_a", [P, NT, E])
        gate_b = sb("gate_b", [P, NT, E])
        logits = sb("logits", [P, NT, E])
        col_a = sb("col_a", [P, NT])
        col_b = sb("col_b", [P, NT])
        gate_T = sb("gate_T", [E, NT * P])
        hidden = sb("hidden", [P, 2, HC, BANK])
        y = sb("y", [P, NT, D])

        x_loaded, mask_loaded, tail_loaded, biases_loaded = map(sem, ("x_loaded", "mask_loaded", "tail_loaded", "biases_loaded"))
        wq_loaded, wk_loaded, wv_loaded, wo_loaded = map(sem, ("wq_loaded", "wk_loaded", "wv_loaded", "wo_loaded"))
        moe_loaded = sem("moe_loaded")
        consts_made, cleared = sem("consts_made"), sem("cleared")
        var_ready, rstd_ready, normed_ready = sem("var_ready"), sem("rstd_ready"), sem("normed_ready")
        pre_filled, pre_drained = sem("pre_filled"), sem("pre_drained")
        far_min_ready = sem("far_min_ready")
        dve_done = sem("dve_done")
        x1_ready = sem("x1_ready")
        flag_ready = sem("flag_ready")
        hid_filled, hid_drained = sem("hid_filled"), sem("hid_drained")
        y_filled, y_drained = sem("y_filled"), sem("y_drained")
        probs_exp = sem("probs_exp")
        shift_ready = sem("shift_ready")
        stored = sem("stored")

        def semaphores(name):
            return {signal: sem(f"{name}_{signal}") for signal in (
                "ctx_loaded", "mask_ready", "filled", "drained", "scored", "max_ready",
                "exp_done", "inv_ready", "normalised", "out_filled")}

        short, full = semaphores("short"), semaphores("full")

        def heads_a_bank(W):
            return BANK // W

        def groups(W):
            return H // 2 // heads_a_bank(W)

        def stages_before(W, b):
            if W == SK:
                return ([("ctx", b)] + [("k", m) for m in range(FT)] + [("v", m) for m in range(FT)]
                        + ([("q", b, m) for m in range(0, FT, 2)] if b else [])
                        + [("vo", b, r, c) for c in range(H * SK // P // 8) for r in range(2)])
            if b:
                return []
            return ([("ctx", 0)] + [("k", m) for m in range(0, FT, 2)] + [("v", m) for m in range(0, FT, 2)]
                    + [("vo", 0, 0, 0), ("vo", 0, 1, 0)])

        def stages_beside(W, b, j):
            if W == SK or b == B - 1:
                return []
            return ([("q", b + 1, m) for m in (0, 2, 4)] if j == 0 else
                    [("q", b + 1, 6), ("vo", b + 1, 0, 0), ("vo", b + 1, 1, 0)])

        def steps(W):
            held = None
            for b in range(B):
                for stage in stages_before(W, b):
                    yield "stage", stage
                for j in range(QT):
                    for g in range(groups(W)):
                        yield "score", (b, j, g)
                        if g == 0:
                            for stage in stages_beside(W, b, j):
                                yield "stage", stage
                        if held:
                            yield "finish", held
                        held = (b, j, g)
                if W == SK or b == B - 1:
                    yield "finish", held
                    held = None

        def stages_until(W, step):
            count = 0
            for s in steps(W):
                count += {"stage": 1, "score": 0, "finish": 2}[s[0]]
                if s == step:
                    return count

        def number(W, b, j, g):
            return (b * QT + j) * groups(W) + g

        def place(W, n):
            return n // groups(W) // QT, n // groups(W) % QT, n % groups(W)

        block = stack.enter_context(nc.Block())

        @block.sync
        def _(sp):
            sp.dma_start(x_tok[:], x.rearrange("b (p j) d -> p b j d", j=QT)).then_inc(x_loaded, 16)
            sp.dma_start(mask_u8[:], mask[0].rearrange("(p j) k -> p j k", j=QT)).then_inc(mask_loaded, 16)
            for r in range(2):
                sp.dma_start(ctx_tail[r * TAIL:(r + 1) * TAIL, :, :],
                             ctx_in.rearrange("(c r) k d -> r k c d", r=2)[r, SK - TAIL:SK, :, :]).then_inc(tail_loaded, 16)
            sp.dma_start(wk_sb[:], Wk).then_inc(wk_loaded, 16)
            sp.dma_start(wv_sb[:], Wv).then_inc(wv_loaded, 16)
            sp.dma_start(wo_sb[:], Wo.rearrange("(m p) d -> p m d", p=P)).then_inc(wo_loaded, 16)
            sp.dma_start(bo_row[:], bo.rearrange("(a d) -> a d", a=1)).then_inc(wo_loaded, 16)
            sp.dma_start(wg_sb[:], w_gate).then_inc(moe_loaded, 16)
            sp.dma_start(bg_row[:], b_gate.rearrange("(a d) -> a d", a=1)).then_inc(moe_loaded, 16)
            sp.dma_start(w1_sb[:], W1.rearrange("e d f -> d e f")).then_inc(moe_loaded, 16)
            sp.dma_start(w2_sb[:], W2.rearrange("e (c p) d -> p e c d", p=P)).then_inc(moe_loaded, 16)
            sp.dma_start(b2_sb[:], b2).then_inc(moe_loaded, 16)
            sp.wait_ge(flag_ready, 1)
            flag = sp.value_load(short_flag[0:1, 0:1], min_val=0, max_val=1)
            with sp.If(flag == 0):
                for b in range(B):
                    if b:
                        sp.wait_ge(full["drained"], stages_until(SK, ("stage", ("ctx", b - 1))))
                    sp.dma_start(ctx_all[:], ctx_in[b].rearrange("(t p) d -> p t d", p=P)).then_inc(full["ctx_loaded"], 16)
            sp.wait_ge(y_drained, 5 + 2 * E)
            sp.dma_start(out.rearrange("b (p j) d -> p b j d", j=QT), y[:].rearrange("p (b j) d -> p b j d", j=QT)).then_inc(stored, 16)
            sp.wait_ge(stored, 16)

        @block.gpsimd
        def _(pool):
            pool.memset(ident[:], 0.0).then_inc(cleared, 1)
            pool.memset(ones[:], 1.0).then_inc(consts_made, 1)
            pool.memset(minus_half[:], -0.5).then_inc(consts_made, 1)
            pool.wait_ge(cleared, 1)
            pool.affine_select(out=ident[:], in_=ident[:], compare_op=ALU.not_equal, fill=1.0, base=0,
                               pattern=[[-1, P]], channel_multiplier=1).then_inc(consts_made, 1)
            pool.iota(iota8[:], [[0, NT], [1, E]], base=0, channel_multiplier=0,
                      allow_small_or_imprecise_dtypes=True).then_inc(consts_made, 1)
            pool.wait_ge(consts_made, 4)
            pool.tensor_copy(ident_bf[:], ident[:]).then_inc(consts_made, 1)

            def inverse_deviation(n):
                pool.wait_ge(var_ready, n)
                pool.tensor_tensor(rstd[:], var_eps[:], minus_half[:], ALU.pow).then_inc(rstd_ready, 1)

            def attention(W, signals):
                for kind, at in steps(W):
                    if kind != "score":
                        continue
                    n = number(W, *at)
                    for r in range(2):
                        pool.wait_ge(signals["inv_ready"], 2 * n + r + 1)
                        p = probs[:, n % 2, r, :].rearrange("p (h w) -> p h w", w=W)
                        inv = inv_sum[:, n % 2, r, 0:heads_a_bank(W)].unsqueeze(2).to_broadcast([P, heads_a_bank(W), W])
                        pool.tensor_tensor(p, p, inv, ALU.mult).then_inc(signals["normalised"], 1)

            inverse_deviation(1)
            pool.wait_ge(flag_ready, 1)
            flag = pool.value_load(short_flag[0:1, 0:1], min_val=0, max_val=1)
            with pool.If(flag == 1):
                attention(TAIL, short)
            with pool.Else():
                attention(SK, full)
            inverse_deviation(2)

        @block.scalar
        def _(act):
            act.dma_start(bias_rows[0:FT, :], bq.rearrange("(m p) -> m p", p=P)).then_inc(biases_loaded, 16)
            act.dma_start(bias_rows[FT:2 * FT, :], bk.rearrange("(m p) -> m p", p=P)).then_inc(biases_loaded, 16)
            act.dma_start(bias_rows[2 * FT:3 * FT, :], bv.rearrange("(m p) -> m p", p=P)).then_inc(biases_loaded, 16)
            act.dma_start(bias_rows[3 * FT:NB, :], b1.rearrange("e (c p) -> (e c) p", p=P)).then_inc(biases_loaded, 16)
            act.dma_start(wq_sb[:], Wq).then_inc(wq_loaded, 16)

            def attention(W, signals):
                for kind, at in steps(W):
                    if kind != "score":
                        continue
                    n = number(W, *at)
                    for r in range(2):
                        act.wait_ge(signals["max_ready"], 2 * n + r + 1)
                        if n >= 2:
                            act.wait_ge(signals["filled"], stages_until(W, ("finish", place(W, n - 2))))
                        for i in range(heads_a_bank(W)):
                            c = slice(i * W, (i + 1) * W)
                            last = act.activation(probs[:, n % 2, r, c], score_bank[n % 2][r][:, c], ACT.Exp,
                                                  bias=neg_max[:, n % 2, r, i:i + 1],
                                                  accum_out=row_sum[:, n % 2, r, i:i + 1])
                        last.then_inc(signals["exp_done"], 1)

            act.wait_ge(flag_ready, 1)
            flag = act.value_load(short_flag[0:1, 0:1], min_val=0, max_val=1)
            with act.If(flag == 1):
                attention(TAIL, short)
            with act.Else():
                attention(SK, full)
            act.wait_ge(shift_ready, 1)
            act.activation(gate_e[:], gate_a[:], ACT.Exp).then_inc(probs_exp, 1)
            for e in range(E):
                for half in range(2):
                    for c in range(HC):
                        n = (e * 2 + half) * HC + c
                        act.wait_ge(hid_filled, n + 1)
                        if e:
                            act.wait_ge(y_filled, 5 + (e - 1) * 2 + half)
                        act.activation(hidden[:, half, c, :], banks[n % 4][:], ACT.Relu,
                                       bias=bias_T[:, 3 * FT + e * HC + c:3 * FT + e * HC + c + 1]).then_inc(hid_drained, 1)

        @block.tensor
        def _(pe):
            def q_job(bank, b, m0):
                for m in range(m0, m0 + 2):
                    last = pe.matmul(bank[:, (m - m0) * S:(m - m0 + 1) * S], wq_sb[:, m * P:(m + 1) * P],
                                     normed_T[:, b * S:(b + 1) * S], start=True, stop=True)
                return last

            pe.wait_ge(consts_made, 5)
            pe.wait_ge(biases_loaded, 64)
            pe.transpose(ring_bank[0][:, 0:NB], bias_rows[:], ident[0:NB, 0:NB]).then_inc(pre_filled, 1)
            pe.wait_ge(far_min_ready, 1)
            pe.matmul(ring_bank[1][0:1, 0:1], far_min[:], ones[:, 0:1], start=True, stop=True).then_inc(pre_filled, 1)
            pe.wait_ge(normed_ready, 1)
            for c in range(2):
                for t in range(4):
                    last = pe.transpose(banks[c][:, t * P:(t + 1) * P], normed[:, c * 4 + t, :], ident[:])
                last.then_inc(pre_filled, 1)
            pe.wait_ge(wq_loaded, 16)
            for i, m in enumerate(range(0, FT, 2)):
                if i == 0:
                    pe.wait_ge(pre_drained, 4)
                if i == 3:
                    pe.wait_ge(pre_drained, 5)
                q_job([banks[6], banks[2], banks[3], banks[6]][i], 0, m).then_inc(pre_filled, 1)

            def attention(W, signals):
                jobs = 0

                def claim():
                    nonlocal jobs
                    jobs += 1
                    if jobs > 3:
                        pe.wait_ge(signals["drained"], jobs - 3)
                    return ring_bank[(jobs - 1) % 3]

                def head(matrix, h, columns):
                    return matrix[(h % 2) * DH:(h % 2 + 1) * DH, h // 2, columns]

                def job_kv(weights, m0):
                    bank = claim()
                    width = SK if W == SK else B * W
                    for i in range(BANK // width):
                        m = m0 + i
                        last = pe.matmul(bank[:, i * width:(i + 1) * width], weights[:, m * P:(m + 1) * P],
                                         ctx_T[:, 0:width], start=True, stop=True)
                    last.then_inc(signals["filled"], 1)

                def job(what):
                    if what[0] == "ctx":
                        bank = claim()
                        if W == SK:
                            pe.wait_ge(signals["ctx_loaded"], 16 * (what[1] + 1))
                            for t in range(SK // P):
                                last = pe.transpose(bank[:, t * P:(t + 1) * P], ctx_all[:, t, :], ident[:])
                            last.then_inc(signals["filled"], 1)
                        else:
                            pe.wait_ge(tail_loaded, 32)
                            for t in range(2):
                                last = pe.transpose(bank[:, t * P:(t + 1) * P], ctx_tail[:, t, :], ident[:])
                            last.then_inc(signals["filled"], 1)
                    elif what[0] in "kv":
                        if what[0] == "k" and what[1] == 0:
                            pe.wait_ge(wk_loaded, 16)
                            pe.wait_ge(signals["drained"], jobs)
                        if what[0] == "v" and what[1] == 0:
                            pe.wait_ge(wv_loaded, 16)
                        job_kv(wk_sb if what[0] == "k" else wv_sb, what[1])
                    elif what[0] == "q":
                        q_job(claim(), what[1], what[2]).then_inc(signals["filled"], 1)
                    elif what[0] == "vo":
                        _, b, r, c = what
                        if r == 1:
                            return
                        if not W == SK and b == 0 or W == SK and c == 0:
                            pe.wait_ge(signals["drained"], jobs)
                            pe.wait_ge(wo_loaded, 32)
                        pair = [claim(), claim()]
                        sub = max(1, P // W)
                        for k in range(4):
                            for i in range(sub):
                                for parity in range(2):
                                    blk = c * 4 + k
                                    hh = blk * P // W + i
                                    keys = min(W, P)
                                    k0 = (0 if W == SK else b * W) + (blk * P % W)
                                    rows = slice(i * W, i * W + keys)
                                    last = pe.matmul(pair[parity][rows, k * D:(k + 1) * D],
                                                     head(v_T, 2 * hh + parity, slice(k0, k0 + keys)),
                                                     head(wo_sb, 2 * hh + parity, slice(0, D)),
                                                     start=True, stop=True, skip_group_check=True)
                                    if k == 3 and i == sub - 1:
                                        last.then_inc(signals["filled"], 1)

                def score(b, j, g):
                    n = number(W, b, j, g)
                    if n == 0:
                        pe.wait_ge(signals["mask_ready"], 1)
                    if n >= 2:
                        pe.wait_ge(signals["exp_done"], 2 * (n - 1))
                    if g == 0 and j == 0:
                        if b == 0:
                            pe.wait_ge(pre_drained, 8)
                        pe.wait_ge(signals["drained"], jobs)
                    for r in range(2):
                        pe.matmul(score_bank[n % 2][r][:], ident_bf[:], mask_bias[:, j, :],
                                  start=True, stop=False, skip_group_check=True)
                    k0 = 0 if W == SK else b * W
                    for i in range(heads_a_bank(W)):
                        for r in range(2):
                            h = 2 * (g * heads_a_bank(W) + i) + r
                            last = pe.matmul(score_bank[n % 2][r][:, i * W:(i + 1) * W],
                                             q_T[(h % 2) * DH:(h % 2 + 1) * DH, b % 2, h // 2, j * P:(j + 1) * P],
                                             head(k_T, h, slice(k0, k0 + W)),
                                             start=False, stop=i == heads_a_bank(W) - 1, skip_group_check=True)
                    last.then_inc(signals["scored"], 1)

                def finish(b, j, g):
                    n = number(W, b, j, g)
                    for r in range(2):
                        pe.wait_ge(signals["normalised"], 2 * n + r + 1)
                        bank = claim()
                        for k in range(4):
                            last = pe.transpose(bank[:, k * P:(k + 1) * P], probs[:, n % 2, r, k * P:(k + 1) * P], ident[:])
                        last.then_inc(signals["filled"], 1)
                    if g == 0:
                        if b or j:
                            pe.wait_ge(x1_ready, b * QT + j)
                        if j == 0:
                            pe.wait_ge(signals["drained"], jobs - 2)
                        pe.matmul(out_bank[:, 0:D], ones[0:1, :], bo_row[:], start=True, stop=False)
                    base = 0 if W == SK else (b % 2) * 8
                    for r in range(2):
                        pe.wait_ge(signals["drained"], jobs - 1 + r)
                        for k in range(4):
                            done = g == groups(W) - 1 and r == 1 and k == 3
                            last = pe.matmul(out_bank[:, 0:D], probs_T[:, r, k * P:(k + 1) * P],
                                             vo[:, base + r * 4 * groups(W) + g * 4 + k, :], start=False, stop=done)
                    last.then_inc(signals["out_filled"], 1)

                for kind, at in steps(W):
                    if kind == "stage":
                        job(at)
                    elif kind == "score":
                        score(*at)
                    else:
                        finish(*at)

            pe.wait_ge(flag_ready, 1)
            flag = pe.value_load(short_flag[0:1, 0:1], min_val=0, max_val=1)
            with pe.If(flag == 1):
                attention(TAIL, short)
            with pe.Else():
                attention(SK, full)

            pe.wait_ge(normed_ready, 2)
            for c in range(2):
                for t in range(4):
                    last = pe.transpose(ring_bank[c][:, t * P:(t + 1) * P], normed[:, c * 4 + t, :], ident[:])
                last.then_inc(y_filled, 1)
            pe.wait_ge(moe_loaded, 80)
            pe.wait_ge(y_drained, 2)
            for t in range(NT):
                pe.matmul(ring_bank[2][:, t * E:(t + 1) * E], ones[0:1, :], bg_row[:], start=True, stop=False)
                last = pe.matmul(ring_bank[2][:, t * E:(t + 1) * E], normed_T[:, t * P:(t + 1) * P], wg_sb[:],
                                 start=False, stop=True)
            last.then_inc(y_filled, 1)

            def hidden_of(e, half):
                for c in range(HC):
                    n = (e * 2 + half) * HC + c
                    if n >= 4:
                        pe.wait_ge(hid_drained, n - 3)
                    pe.matmul(banks[n % 4][:], w1_sb[:, e, c * P:(c + 1) * P], normed_T[:, half * BANK:(half + 1) * BANK],
                              start=True, stop=True).then_inc(hid_filled, 1)

            def output_of(e, half):
                n = 4 + e * 2 + half
                pe.wait_ge(hid_drained, (e * 2 + half + 1) * HC)
                pe.wait_ge(y_drained, max(n - 1, 4))
                for t in range(4):
                    for c in range(HC):
                        last = pe.matmul(banks[6 + n % 2][:, t * D:(t + 1) * D], hidden[:, half, c, t * P:(t + 1) * P],
                                         w2_sb[:, e, c, :], start=(c == 0), stop=(c == HC - 1))
                last.then_inc(y_filled, 1)

            hidden_of(0, 0)
            pe.wait_ge(y_drained, 3)
            for t in range(NT):
                last = pe.transpose(ring_bank[t // 4][0:E, (t % 4) * P:(t % 4 + 1) * P], gate_b[:, t, :], ident[:])
            last.then_inc(y_filled, 1)
            for e in range(E):
                for half in range(2):
                    if e or half:
                        hidden_of(e, half)
                        prev = (e * 2 + half - 1)
                        output_of(prev // 2, prev % 2)
            output_of(E - 1, 1)
            pe.wait_ge(y_drained, 4 + 2 * E)
            for t in range(NT):
                last = pe.matmul(banks[4 + t // 4][:, (t % 4) * D:(t % 4 + 1) * D], gate_T[:, t * P:(t + 1) * P], b2_sb[:],
                                 start=True, stop=True)
            last.then_inc(y_filled, 1)

        @block.vector
        def _(dve):
            links = 0

            def after(instruction):
                nonlocal links
                links += 1
                instruction.then_inc(dve_done, 1)
                dve.wait_ge(dve_done, links)

            def layernorm(src, round_):
                for t in range(NT):
                    last = dve.bn_stats(stats[:, t, :], src[:, t, :])
                after(last)
                for t in range(NT):
                    last = dve.bn_aggr(mean_var[:, t, :], stats[:, t, :])
                after(last)
                dve.tensor_scalar(var_eps[:], mean_var[:, :, 1], EPS, None, ALU.add).then_inc(var_ready, 1)
                dve.wait_ge(rstd_ready, round_)
                for t in range(NT):
                    last = dve.tensor_scalar(normed[:, t, :], src[:, t, :], mean_var[:, t, 0:1], rstd[:, t:t + 1],
                                             ALU.subtract, ALU.mult)
                last.then_inc(normed_ready, 1)

            dve.wait_ge(mask_loaded, 16)
            dve.tensor_reduce(far_min[:], mask_u8[:, :, 0:SK - TAIL], AX.XY, ALU.min).then_inc(far_min_ready, 1)
            after(dve.tensor_reduce(row_min[:], mask_u8[:], AX.X, ALU.min))
            after(dve.tensor_scalar(blown[:], row_min[:], HUGE, HUGE, ALU.mult, ALU.mult))
            after(dve.tensor_tensor(dead_row[:], blown[:], blown[:], ALU.subtract))
            dve.wait_ge(x_loaded, 16)
            x_flat = x_tok[:].rearrange("p b j d -> p (b j) d")
            layernorm(x_flat, 1)
            dve.wait_ge(pre_filled, 1)
            dve.tensor_copy(bias_T[:], ring_bank[0][:, 0:NB]).then_inc(pre_drained, 1)
            dve.wait_ge(pre_filled, 2)
            dve.tensor_scalar(short_flag[:], ring_bank[1][0:1, 0:1], float(P), None, ALU.is_equal).then_inc(flag_ready, 1)
            dve.wait_ge(pre_drained, 1)
            dve.tensor_scalar(bq_scaled[:], bias_T[:, 0:FT], SCALE, None, ALU.mult).then_inc(pre_drained, 1)
            for c in range(2):
                dve.wait_ge(pre_filled, 3 + c)
                dve.tensor_copy(normed_T[:, c * BANK:(c + 1) * BANK], banks[c][:]).then_inc(pre_drained, 1)

            def drain_q(bank, b, m):
                bias = bq_scaled[:, m:m + 2].unsqueeze(2).to_broadcast([P, 2, S])
                return dve.scalar_tensor_tensor(out=q_T[:, b % 2, m:m + 2, :], in0=bank[:].rearrange("p (m s) -> p m s", s=S),
                                                scalar=SCALE, in1=bias, op0=ALU.mult, op1=ALU.add)

            dve.wait_ge(pre_drained, 2)
            for i, m in enumerate(range(0, FT, 2)):
                dve.wait_ge(pre_filled, 5 + i)
                drain_q([banks[6], banks[2], banks[3], banks[6]][i], 0, m).then_inc(pre_drained, 1)

            def attention(W, signals):
                HB = heads_a_bank(W)
                jobs = 0

                tail = mask_u8[:, :, SK - W:SK].unsqueeze(2).to_broadcast([P, QT, HB, W])
                for j in range(QT):
                    last = dve.tensor_scalar(mask_bias[:, j, :].rearrange("p (h w) -> p h w", w=W),
                                             tail[:, j, :, :], MASKED, None, ALU.mult)
                last.then_inc(signals["mask_ready"], 1)

                def next_bank():
                    nonlocal jobs
                    jobs += 1
                    dve.wait_ge(signals["filled"], jobs)
                    return ring_bank[(jobs - 1) % 3]

                def job(what):
                    bank = next_bank()
                    if what[0] == "ctx":
                        width = SK if W == SK else B * W
                        i = dve.tensor_copy(ctx_T[:, 0:width], bank[:, 0:width])
                    elif what[0] in "kv":
                        width = SK if W == SK else B * W
                        many = BANK // width
                        to = k_T if what[0] == "k" else v_T
                        col = (FT if what[0] == "k" else 2 * FT) + what[1]
                        bias = bias_T[:, col:col + many].unsqueeze(2).to_broadcast([P, many, width])
                        i = dve.tensor_tensor(to[:, what[1]:what[1] + many, 0:width],
                                              bank[:].rearrange("p (m s) -> p m s", s=width), bias, ALU.add)
                    elif what[0] == "q":
                        i = drain_q(bank, what[1], what[2])
                    else:
                        _, b, r, c = what
                        base = (0 if W == SK else (b % 2) * 8) + r * 4 * groups(W) + c * 4
                        i = dve.tensor_copy(vo[:, base:base + 4, :], bank[:].rearrange("p (k d) -> p k d", d=D))
                    i.then_inc(signals["drained"], 1)

                def inverse(n):
                    for r in range(2):
                        dve.wait_ge(signals["exp_done"], 2 * n + r + 1)
                        dve.reciprocal(inv_sum[:, n % 2, r, 0:HB], row_sum[:, n % 2, r, 0:HB]).then_inc(signals["inv_ready"], 1)

                last_group = B * QT * groups(W) - 1
                for kind, at in steps(W):
                    if kind == "stage":
                        job(at)
                        continue
                    b, j, g = at
                    n = number(W, b, j, g)
                    if kind == "score":
                        if n and not (W == SK and j == 0 and g == 0):
                            inverse(n - 1)
                        dve.wait_ge(signals["scored"], n + 1)
                        for r in range(2):
                            dve.tensor_reduce(neg_max[:, n % 2, r, 0:HB],
                                              score_bank[n % 2][r][:].rearrange("p (h w) -> p h w", w=W),
                                              AX.X, ALU.max, negate=True).then_inc(signals["max_ready"], 1)
                    else:
                        if n == last_group or (W == SK and j == QT - 1 and g == groups(W) - 1):
                            inverse(n)
                        for r in range(2):
                            dve.tensor_copy(probs_T[:, r, :], next_bank()[:]).then_inc(signals["drained"], 1)
                        if g == groups(W) - 1:
                            dve.wait_ge(signals["out_filled"], n + 1)
                            dve.scalar_tensor_tensor(out=x1[:, b * QT + j, :], in0=out_bank[:, 0:D],
                                                     scalar=dead_row[:, j:j + 1], in1=x_flat[:, b * QT + j, :],
                                                     op0=ALU.add, op1=ALU.add).then_inc(x1_ready, 1)

            dve.wait_ge(flag_ready, 1)
            flag = dve.value_load(short_flag[0:1, 0:1], min_val=0, max_val=1)
            with dve.If(flag == 1):
                attention(TAIL, short)
            with dve.Else():
                attention(SK, full)
            dve.wait_ge(x1_ready, NT)
            layernorm(x1, 2)
            for c in range(2):
                dve.wait_ge(y_filled, 1 + c)
                dve.tensor_copy(normed_T[:, c * BANK:(c + 1) * BANK], ring_bank[c][:]).then_inc(y_drained, 1)

            def wide(col):
                return col[:].unsqueeze(2).to_broadcast([P, NT, E])

            dve.wait_ge(y_filled, 3)
            after(dve.tensor_copy(logits[:], ring_bank[2][:, 0:NT * E].rearrange("p (t e) -> p t e", e=E)))
            after(dve.tensor_reduce(col_a[:], logits[:], AX.X, ALU.max))
            dve.tensor_tensor(gate_a[:], logits[:], wide(col_a), ALU.subtract).then_inc(shift_ready, 1)
            dve.wait_ge(probs_exp, 1)
            after(dve.tensor_reduce(col_a[:], gate_e[:], AX.X, ALU.add))
            after(dve.reciprocal(col_b[:], col_a[:]))
            after(dve.tensor_tensor(gate_a[:], gate_e[:], wide(col_b), ALU.mult))
            after(dve.tensor_reduce(col_a[:], gate_a[:], AX.X, ALU.max))
            after(dve.tensor_tensor(gate_b[:], gate_a[:], wide(col_a), ALU.is_equal))
            after(dve.scalar_tensor_tensor(out=gate_e[:], in0=gate_b[:], scalar=-float(E), in1=iota8[:], op0=ALU.mult, op1=ALU.add))
            after(dve.tensor_reduce(col_b[:], gate_e[:], AX.X, ALU.min))
            after(dve.tensor_scalar(col_b[:], col_b[:], float(E), None, ALU.add))
            after(dve.tensor_tensor(gate_e[:], iota8[:], wide(col_b), ALU.is_equal))
            dve.tensor_tensor(gate_b[:], gate_e[:], wide(col_a), ALU.mult).then_inc(y_drained, 1)
            dve.wait_ge(y_filled, 4)
            for c in range(2):
                last = dve.tensor_copy(gate_T[:, c * BANK:(c + 1) * BANK], ring_bank[c][0:E, :])
            last.then_inc(y_drained, 1)
            for e in range(E):
                for half in range(2):
                    n = 4 + e * 2 + half
                    dve.wait_ge(y_filled, n + 1)
                    dve.wait_ge(y_drained, n)
                    for t in range(4):
                        tt = half * 4 + t
                        last = dve.scalar_tensor_tensor(out=y[:, tt, :], in0=banks[6 + n % 2][:, t * D:(t + 1) * D],
                                                        scalar=gate_b[:, tt, e:e + 1], in1=(y if e else x1)[:, tt, :],
                                                        op0=ALU.mult, op1=ALU.add)
                    last.then_inc(y_drained, 1)
            n = 4 + 2 * E
            dve.wait_ge(y_filled, n + 1)
            dve.wait_ge(y_drained, n)
            for c in range(2):
                yy = y[:, c * 4:(c + 1) * 4, :]
                last = dve.tensor_tensor(yy, banks[4 + c][:].rearrange("p (t d) -> p t d", d=D), yy, ALU.add)
            last.then_inc(y_drained, 1)


_INS = ["x", "ctx_1024", "mask_1xSxS2_bk1", "L0_xattn_Wq", "L0_xattn_bq", "L0_xattn_Wk", "L0_xattn_bk",
        "L0_xattn_Wv", "L0_xattn_bv", "L0_xattn_Wo", "L0_xattn_bo", "L0_ffn_w_gate", "L0_ffn_b_gate",
        "L0_ffn_W1", "L0_ffn_b1", "L0_ffn_W2", "L0_ffn_b2"]


def kernel(**inputs):
    import numpy as np
    import concourse.bacc as bacc
    from concourse import mybir as _mybir
    from concourse.bass_utils import run_bass_kernel_spmd

    nc = bacc.Bacc("TRN2", target_bir_lowering=False, num_devices=1)
    arrays, args = {}, []
    for name in _INS:
        a = np.ascontiguousarray(inputs[name])
        arrays[f"in_{name}"] = a
        args.append(nc.dram_tensor(f"in_{name}", a.shape, _mybir.dt.from_np(a.dtype), kind="ExternalInput").ap())
    shape = arrays["in_x"].shape
    args.append(nc.dram_tensor("out_x", shape, _mybir.dt.float32, kind="ExternalOutput").ap())
    xattn_moe(nc, *args)
    r = run_bass_kernel_spmd(nc, [arrays], core_ids=[0])
    return np.asarray(r.results[0]["out_x"])
```

```python
from contextlib import ExitStack

import concourse.bass as bass
from concourse import mybir
from concourse.alu_op_type import AluOpType as ALU

ACT = mybir.ActivationFunctionType
AX = mybir.AxisListType
F32 = mybir.dt.float32
BF16 = mybir.dt.bfloat16
I32 = mybir.dt.int32
U8 = mybir.dt.uint8

P = 128
BANK = 512
TAIL = 64
MASKED = -1e30
HUGE = 3e38
EPS = 1e-5



def xattn_moe(nc, x, ctx_in, mask, Wq, bq, Wk, bk, Wv, bv, Wo, bo,
              w_gate, b_gate, W1, b1, W2, b2, out):
    B, S, D = x.shape
    SK = ctx_in.shape[1]
    HD = Wq.shape[1]
    DH = 64
    H = HD // DH
    E = w_gate.shape[1]
    F = W1.shape[2]
    QT = S // P
    NT = B * QT
    N = NT * P
    FT = HD // P
    HC = F // P
    SCALE = DH ** -0.5
    MEAN, RSTD, PROB, INDEX = D, D + 1, D + 2, D + 3
    ROW = D + 4
    TILES = NT + E - 1
    SPARE = TILES - NT
    DVE_ZEROS = FT * SK * 5 // 8
    assert D == P and FT * 2 == H and QT == 2 and F == BANK and SPARE * P <= N

    with ExitStack() as stack:
        def sb(name, shape, dt=F32):
            return stack.enter_context(nc.sbuf_tensor(name, shape, dt))

        def sem(name):
            return stack.enter_context(nc.semaphore(name))

        banks = [stack.enter_context(nc.psum_tensor(f"bank{i}", [P, BANK], F32)) for i in range(8)]
        score_bank = [[banks[0], banks[1]], [banks[2], banks[3]]]
        turn_bank = [banks[4], banks[5]]
        work_bank = banks[6]
        out_bank = banks[7]
        x_bank = turn_bank
        q0_bank = banks[0:4]

        x_tok = sb("x_tok", [P, B, QT, D])
        mask_u8 = sb("mask_u8", [P, QT, SK], U8)
        ctx_tail = sb("ctx_tail", [P, 2, D])
        ctx_all = sb("ctx_all", [P, SK // P, D])
        wq_sb = sb("wq_sb", [P, HD])
        wk_sb = sb("wk_sb", [P, HD])
        wv_sb = sb("wv_sb", [P, HD])
        wo_sb = sb("wo_sb", [P, FT, D])
        bo_wide = sb("bo_wide", [P, 1, D])
        NB = 3 * FT + E * HC
        bias_rows = sb("bias_rows", [NB, P])
        wg_sb = sb("wg_sb", [P, E])
        bg_wide = sb("bg_wide", [P, 1, E])
        w1_sb = sb("w1_sb", [P, E, F])
        w2_sb = sb("w2_sb", [P, E, HC * D])
        b2_wide = sb("b2_wide", [P, E, D])

        ident = sb("ident", [P, P])
        ident_bf = sb("ident_bf", [P, P], BF16)
        ones = sb("ones", [P, P])
        ones_bf = sb("ones_bf", [P, P], BF16)
        before = sb("before", [P, P], BF16)
        minus_half = sb("minus_half", [P, NT])
        falling = sb("falling", [P, QT, E])
        thresholds = sb("thresholds", [1, E, E])
        upto = sb("upto", [1, E, E])
        tile_index = sb("tile_index", [1, TILES, E])
        tile_row = sb("tile_row", [1, TILES])
        empty_row = sb("empty_row", [P, 1, ROW])

        stats = sb("stats", [P, NT, nc.vector.BN_STATS_DIM])
        mean_var = sb("mean_var", [P, NT, nc.vector.BN_AGGR_DIM])
        var_eps = sb("var_eps", [P, NT])
        rstd = sb("rstd", [P, NT])
        normed = sb("normed", [P, NT, D])
        normed_T = sb("normed_T", [P, N])
        x_bo = sb("x_bo", [P, NT, D])
        bias_T = sb("bias_T", [P, NB])
        bq_scaled = sb("bq_scaled", [P, FT])
        row_min = sb("row_min", [P, QT])
        far_min = sb("far_min", [P, 1])
        blown = sb("blown", [P, QT])
        dead_row = sb("dead_row", [P, QT])
        short_flag = sb("short_flag", [1, 1], I32)

        mask_bias = sb("mask_bias", [P, QT, BANK], BF16)
        ctx_T = sb("ctx_T", [P, BANK])
        q_T = sb("q_T", [P, 2, FT, S])
        zero_padded = sb("zero_padded", [P, FT * 2 * SK])
        k_short, v_short = (zero_padded[:, i * FT * B * 2 * TAIL:(i + 1) * FT * B * 2 * TAIL].rearrange(
            "p (m b r k) -> p m b r k", m=FT, b=B, r=2) for i in range(2))
        kv_full = zero_padded[:].rearrange("p (m r k) -> p m r k", m=FT, r=2)
        VO_BLOCKS = H * SK // P
        vo = sb("vo", [P, VO_BLOCKS, D])
        neg_max = sb("neg_max", [P, 2, 2, 8])
        row_sum = sb("row_sum", [P, 2, 2, 8])
        inv_sum = sb("inv_sum", [P, 2, 2, 8])
        probs = sb("probs", [P, 2, 2, BANK])
        probs_T = sb("probs_T", [P, 2, BANK])

        stats2 = sb("stats2", [P, QT, nc.vector.BN_STATS_DIM])
        mean_var2 = sb("mean_var2", [P, QT, nc.vector.BN_AGGR_DIM])
        var_eps2 = sb("var_eps2", [P, QT])
        rstd2 = sb("rstd2", [P, QT])
        token_rows = sb("token_rows", [P, NT, ROW])
        normed2 = sb("normed2", [P, QT, D])
        normed2_T = sb("normed2_T", [P, S])
        logits = sb("logits", [P, QT, E])
        below_max = sb("below_max", [P, QT, E])
        exps = sb("exps", [P, QT, E])
        gate_neg_max = sb("gate_neg_max", [P, QT])
        gate_sum = sb("gate_sum", [P, QT])
        candidates = sb("candidates", [P, QT, E])
        chosen = sb("chosen", [P, QT])
        onehot = sb("onehot", [P, QT, E], BF16)
        seen = sb("seen", [P, E], BF16)
        ranks = sb("ranks", [P, QT, E])
        rank = sb("rank", [P, QT])
        row_of = sb("row_of", [P, NT], I32)

        counts = sb("counts", [1, E])
        pairs = sb("pairs", [1, E, E])
        tiles_of = sb("tiles_of", [1, E])
        end_of = sb("end_of", [1, E])
        passed = sb("passed", [1, TILES, E])
        passed_tiles = sb("passed_tiles", [1, TILES, E])
        expert_f = sb("expert_f", [1, TILES])
        first_f = sb("first_f", [1, TILES])
        row_f = sb("row_f", [1, TILES])
        expert_of = sb("expert_of", [1, TILES], I32)
        first_row = sb("first_row", [1, TILES], I32)
        used_tiles = sb("used_tiles", [1, 1], I32)

        assert VO_BLOCKS * D >= TILES * (ROW + P + 2 * D) + 2 * D and FT * 2 * SK >= 5 * F
        flat = vo[:].rearrange("p t d -> p (t d)")
        tile_rows = flat[:, 0:TILES * ROW].rearrange("p (t d) -> p t d", d=ROW)
        rows_T = flat[:, TILES * ROW:TILES * (ROW + P)]
        slot_normed = flat[:, TILES * (ROW + P):TILES * (ROW + P + D)].rearrange("p (t d) -> p t d", d=D)
        plus_b2 = flat[:, TILES * (ROW + P + 2 * D):TILES * (ROW + P + 2 * D) + 2 * D].rearrange("p (t d) -> p t d", d=D)
        results = flat[:, TILES * (ROW + P + D):TILES * (ROW + P + 2 * D)].rearrange("p (t d) -> p t d", d=D)
        w1_stage = zero_padded[:, 0:3 * F].rearrange("p (i f) -> p i f", i=3)
        hidden = zero_padded[:, 3 * F:5 * F].rearrange("p (i f) -> p i f", i=2)
        b1_stage = sb("b1_stage", [P, 3, HC])
        token_of = sb("token_of", [P, TILES], I32)

        out_rows = out.rearrange("b s d -> (b s) d")
        regions = nc.dram_tensor("regions", [(E + 1) * N, ROW], F32).ap()

        x_loaded, mask_loaded, tail_loaded, biases_loaded = map(sem, ("x_loaded", "mask_loaded", "tail_loaded", "biases_loaded"))
        wq_loaded, wk_loaded, wv_loaded, wo_loaded, bo_loaded = map(sem, ("wq_loaded", "wk_loaded", "wv_loaded", "wo_loaded", "bo_loaded"))
        router_loaded, experts_loaded = sem("router_loaded"), sem("experts_loaded")
        cleared, consts_made, more_consts = sem("cleared"), sem("consts_made"), sem("more_consts")
        var_ready, rstd_ready, normed_ready, x_bo_ready = map(sem, ("var_ready", "rstd_ready", "normed_ready", "x_bo_ready"))
        bias_filled, bias_ready, flag_filled = sem("bias_filled"), sem("bias_ready"), sem("flag_filled")
        x_filled, x_drained, q0_filled, q0_drained = map(sem, ("x_filled", "x_drained", "q0_filled", "q0_drained"))
        far_min_ready, flag_ready, zeros_ready = sem("far_min_ready"), sem("flag_ready"), sem("zeros_ready")
        dve_done = sem("dve_done")
        x1_ready = sem("x1_ready")
        var2_ready, rstd2_ready, h_ready = sem("var2_ready"), sem("rstd2_ready"), sem("h_ready")
        router_filled, router_drained = sem("router_filled"), sem("router_drained")
        gate_max_ready, gate_sum_ready = sem("gate_max_ready"), sem("gate_sum_ready")
        onehot_ready, seen_ready, rows_ready, table_ready = map(sem, ("onehot_ready", "seen_ready", "rows_ready", "table_ready"))
        regions_cleared, scattered = sem("regions_cleared"), sem("scattered")
        tile_loaded = [sem(f"tile_loaded{i}") for i in range(TILES)]
        slot_ready, turned, turn_drained = sem("slot_ready"), sem("turned"), sem("turn_drained")
        staged, hid_filled, relu_done = sem("staged"), sem("hid_filled"), sem("relu_done")
        y_filled, plus_ready, result_ready, result_scattered = map(sem, ("y_filled", "plus_ready", "result_ready", "result_scattered"))
        tokens_ready = sem("tokens_ready")

        def semaphores(name):
            return {signal: sem(f"{name}_{signal}") for signal in (
                "ctx_loaded", "mask_ready", "filled", "drained", "odd_drained", "scored", "max_ready",
                "exp_done", "inv_ready", "normalised", "turn_filled", "turn_drained", "out_filled", "dve_done")}

        short, full = semaphores("short"), semaphores("full")

        def heads_a_bank(W):
            return BANK // W

        def groups(W):
            return H // 2 // heads_a_bank(W)

        def number(W, b, j, g):
            return (b * QT + j) * groups(W) + g

        def steps(W):
            rotation = [work_bank, turn_bank[0], turn_bank[1]]
            turn = 0

            def rotating(stages):
                nonlocal turn
                for stage in stages:
                    yield "work", stage, rotation[turn % 3]
                    turn += 1

            keys = [("k", m) for m in range(0, FT, 1 if W == SK else 2)]
            values = [("v", m) for m in range(0, FT, 1 if W == SK else 2)]
            held = None
            for b in range(B):
                if W == SK:
                    room = []
                    yield from rotating([("ctx", b)] + values + [("vo", b, c) for c in range(2 * groups(W))] + keys)
                    if b:
                        yield from rotating([("q", b, m) for m in range(0, FT, 2)])
                else:
                    room = [("vo", b, 0), ("vo", b, 1)] + [("q", b + 1, m) for m in range(0, FT, 2) if b + 1 < B]
                    if b == 0:
                        yield from rotating([("ctx", 0)] + keys)
                for j in range(QT):
                    for g in range(groups(W)):
                        now = (b, j, g)
                        yield "score", now
                        yield "exp", now, 0
                        if W != SK and b == 0 and j == 0:
                            yield from rotating(values[:2])
                            yield "exp", now, 1
                            yield from rotating(values[2:])
                        else:
                            yield "exp", now, 1
                        if held:
                            yield "turn", held, 0
                            yield "turn", held, 1
                        if g == 0 and j == 1 and b >= 1:
                            yield "normalise", b - 1
                        if room:
                            yield "work", room.pop(0), work_bank
                        yield "inverse", now, 0
                        if held:
                            yield "out", held
                        if g == 0 and j == 1 and b >= 1:
                            yield "h_T", b - 1
                        if g == 0 and j == 0 and b >= 2:
                            yield "rank", b - 2
                        if room:
                            yield "work", room.pop(0), turn_bank[0]
                        if g == 0 and j == 0 and b >= 1 and W != SK:
                            yield "ln2", b - 1
                        yield "inverse", now, 1
                        if room:
                            yield "work", room.pop(0), turn_bank[1]
                        if g == 0 and j == 1 and b >= 1:
                            yield "logits", b - 1
                        held = now
                if W == SK or b == B - 1:
                    yield "turn", held, 0
                    yield "turn", held, 1
                    if b == B - 1:
                        yield "rank", b - 1
                    yield "out", held
                    if b < B - 1:
                        yield "ln2", b
                    held = None

        def work_until(W, stage):
            count = 0
            for kind, at, *_ in steps(W):
                count += kind == "work"
                if kind == "work" and at == stage:
                    return count

        block = stack.enter_context(nc.Block())

        @block.sync
        def _(sp):
            sp.dma_start(x_tok[:], x.rearrange("b (p j) d -> p b j d", j=QT)).then_inc(x_loaded, 16)
            sp.dma_start(mask_u8[:], mask[0].rearrange("(p j) k -> p j k", j=QT)).then_inc(mask_loaded, 16)
            for r in range(2):
                sp.dma_start(ctx_tail[r * TAIL:(r + 1) * TAIL, :, :],
                             ctx_in.rearrange("(c r) k d -> r k c d", r=2)[r, SK - TAIL:SK, :, :]).then_inc(tail_loaded, 16)
            sp.dma_start(wk_sb[:], Wk).then_inc(wk_loaded, 16)
            sp.dma_start(wv_sb[:], Wv).then_inc(wv_loaded, 16)
            sp.dma_start(wo_sb[:], Wo.rearrange("(m p) d -> p m d", p=P)).then_inc(wo_loaded, 16)
            sp.dma_start(wg_sb[:], w_gate).then_inc(router_loaded, 16)
            sp.dma_start(bg_wide[:], b_gate.partition_broadcast(P).unsqueeze(1)).then_inc(router_loaded, 16)
            sp.wait_ge(more_consts, 2)
            sp.dma_start(regions[0:SPARE * P, :].rearrange("(t p) d -> p t d", p=P),
                         empty_row[:].to_broadcast([P, SPARE, ROW])).then_inc(regions_cleared, 16)
            sp.dma_start(regions[N:(E + 1) * N, :].rearrange("(t p) d -> p t d", p=P),
                         empty_row[:].to_broadcast([P, E * NT, ROW])).then_inc(regions_cleared, 16)
            sp.dma_start(w1_sb[:], W1.rearrange("e d f -> d e f")).then_inc(experts_loaded, 16)
            sp.dma_start(w2_sb[:].rearrange("p e (c d) -> p e c d", d=D),
                         W2.rearrange("e (c p) d -> p e c d", p=P)).then_inc(experts_loaded, 16)
            sp.dma_start(b2_wide[:], b2.partition_broadcast(P)).then_inc(experts_loaded, 16)
            sp.wait_ge(flag_ready, 1)
            flag = sp.value_load(short_flag[0:1, 0:1], min_val=0, max_val=1)
            with sp.If(flag == 0):
                for b in range(B):
                    if b:
                        sp.wait_ge(full["drained"], work_until(SK, ("ctx", b - 1)))
                    sp.dma_start(ctx_all[:], ctx_in[b].rearrange("(t p) d -> p t d", p=P)).then_inc(full["ctx_loaded"], 16)
            sp.wait_ge(table_ready, 1)
            sp.wait_ge(scattered, 16 * NT)
            for i in range(TILES):
                row = sp.value_load(first_row[0:1, i:i + 1], min_val=0, max_val=(E + 1) * N - P)
                sp.dma_start(tile_rows[:, i, :], regions[bass.ds(row, P), :]).then_inc(tile_loaded[i], 16)

        @block.gpsimd
        def _(pool):
            pool.memset(ident[:], 0.0).then_inc(cleared, 1)
            pool.memset(ones[:], 1.0).then_inc(consts_made, 1)
            pool.memset(minus_half[:], -0.5).then_inc(consts_made, 1)
            pool.wait_ge(cleared, 1)
            pool.affine_select(out=ident[:], in_=ident[:], compare_op=ALU.not_equal, fill=1.0, base=0,
                               pattern=[[-1, P]], channel_multiplier=1).then_inc(consts_made, 1)
            pool.memset(zero_padded[:, 0:FT * SK], 0.0).then_inc(zeros_ready, 1)
            pool.memset(zero_padded[:, FT * SK + DVE_ZEROS:2 * FT * SK], 0.0).then_inc(zeros_ready, 1)

            pool.wait_ge(consts_made, 3)
            pool.wait_ge(var_ready, 1)
            pool.tensor_tensor(rstd[:], var_eps[:], minus_half[:], ALU.pow).then_inc(rstd_ready, 1)
            pool.tensor_copy(ident_bf[:], ident[:]).then_inc(consts_made, 1)

            pool.memset(empty_row[:], 0.0).then_inc(cleared, 1)
            pool.memset(ones_bf[:], 1.0).then_inc(more_consts, 1)
            pool.wait_ge(cleared, 2)
            pool.memset(empty_row[:, :, INDEX], float(N)).then_inc(more_consts, 1)
            pool.iota(falling[:], [[0, QT], [-1, E]], base=E, channel_multiplier=0,
                      allow_small_or_imprecise_dtypes=True).then_inc(more_consts, 1)
            pool.iota(thresholds[:], [[0, E], [P, E]], base=0, channel_multiplier=0,
                      allow_small_or_imprecise_dtypes=True).then_inc(more_consts, 1)
            pool.iota(tile_index[:], [[1, TILES], [0, E]], base=0, channel_multiplier=0,
                      allow_small_or_imprecise_dtypes=True).then_inc(more_consts, 1)
            pool.iota(tile_row[:], [[P, TILES]], base=E * N, channel_multiplier=0,
                      allow_small_or_imprecise_dtypes=True).then_inc(more_consts, 1)
            pool.iota(token_rows[:, :, INDEX].rearrange("p (b j) -> p b j", j=QT), [[S, B], [1, QT]], base=0,
                      channel_multiplier=QT, allow_small_or_imprecise_dtypes=True).then_inc(more_consts, 1)
            pool.memset(seen[:], 0.0).then_inc(more_consts, 1)
            pool.wait_ge(more_consts, 1)
            pool.affine_select(out=before[:], in_=ones_bf[:], compare_op=ALU.is_gt, fill=0.0, base=0,
                               pattern=[[1, P]], channel_multiplier=-1).then_inc(more_consts, 1)
            pool.affine_select(out=upto[:], in_=ones[0:1, 0:E * E].rearrange("p (e k) -> p e k", k=E), compare_op=ALU.is_ge,
                               fill=0.0, base=0, pattern=[[1, E], [-1, E]], channel_multiplier=0).then_inc(more_consts, 1)
            pool.wait_ge(x_loaded, 16)
            pool.wait_ge(bo_loaded, 16)
            pool.tensor_tensor(x_bo[:], x_tok[:].rearrange("p b j d -> p (b j) d"), bo_wide[:].to_broadcast([P, NT, D]),
                               ALU.add).then_inc(x_bo_ready, 1)

            def second_deviation(b):
                pool.wait_ge(var2_ready, b + 1)
                pool.tensor_tensor(rstd2[:], var_eps2[:], minus_half[:, 0:QT], ALU.pow).then_inc(rstd2_ready, 1)

            def scatter_rows(b):
                if b == 0:
                    pool.wait_ge(regions_cleared, 32)
                pool.wait_ge(rows_ready, b + 1)
                for t in range(QT * b, QT * (b + 1)):
                    pool.indirect_dma_start(out=regions, out_offset=bass.IndirectOffsetOnAxis(ap=row_of[:, t:t + 1], axis=0),
                                            in_=token_rows[:, t, :], in_offset=None).then_inc(scattered, 16)

            def attention(W, signals):
                HB = heads_a_bank(W)
                for j in range(QT):
                    hidden_keys = mask_u8[:, j, SK - W:SK].unsqueeze(1).to_broadcast([P, HB, W])
                    last = pool.tensor_scalar(mask_bias[:, j, :].rearrange("p (h w) -> p h w", w=W),
                                              hidden_keys, MASKED, None, ALU.mult)
                last.then_inc(signals["mask_ready"], 1)
                for kind, at, *rest in steps(W):
                    if kind == "inverse":
                        n, r = number(W, *at), rest[0]
                        pool.wait_ge(signals["inv_ready"], 2 * n + r + 1)
                        p = probs[:, n % 2, r, :].rearrange("p (h w) -> p h w", w=W)
                        inv = inv_sum[:, n % 2, r, 0:HB].unsqueeze(2).to_broadcast([P, HB, W])
                        pool.tensor_tensor(p, p, inv, ALU.mult).then_inc(signals["normalised"], 1)
                    elif kind == "ln2":
                        second_deviation(at)
                    elif kind == "rank":
                        scatter_rows(at)

            pool.wait_ge(flag_ready, 1)
            flag = pool.value_load(short_flag[0:1, 0:1], min_val=0, max_val=1)
            with pool.If(flag == 1):
                attention(TAIL, short)
            with pool.Else():
                attention(SK, full)
            second_deviation(B - 1)
            scatter_rows(B - 1)

            def scatter_result(i):
                pool.wait_ge(tile_loaded[i], 16)
                pool.tensor_copy(token_of[:, i:i + 1], tile_rows[:, i, INDEX:INDEX + 1]).then_inc(tokens_ready, 1)
                pool.wait_ge(tokens_ready, i + 1)
                pool.wait_ge(result_ready, i + 1)
                pool.indirect_dma_start(out=out_rows, out_offset=bass.IndirectOffsetOnAxis(ap=token_of[:, i:i + 1], axis=0),
                                        in_=results[:, i, :], in_offset=None, bounds_check=N - 1,
                                        oob_is_err=False).then_inc(result_scattered, 16)

            def scatter_from(i):
                if i == TILES:
                    pool.wait_ge(result_scattered, 16 * TILES)
                    return
                with pool.If(used > i):
                    scatter_result(i)
                    scatter_from(i + 1)
                with pool.Else():
                    pool.wait_ge(result_scattered, 16 * i)

            pool.wait_ge(table_ready, 1)
            used = pool.value_load(used_tiles[0:1, 0:1], min_val=NT, max_val=TILES)
            for i in range(NT):
                scatter_result(i)
            scatter_from(NT)

        @block.scalar
        def _(act):
            act.dma_start(bias_rows[0:FT, :], bq.rearrange("(m p) -> m p", p=P)).then_inc(biases_loaded, 16)
            act.dma_start(bias_rows[FT:2 * FT, :], bk.rearrange("(m p) -> m p", p=P)).then_inc(biases_loaded, 16)
            act.dma_start(bias_rows[2 * FT:3 * FT, :], bv.rearrange("(m p) -> m p", p=P)).then_inc(biases_loaded, 16)
            act.dma_start(bias_rows[3 * FT:NB, :], b1.rearrange("e (c p) -> (e c) p", p=P)).then_inc(biases_loaded, 16)
            act.dma_start(wq_sb[:], Wq).then_inc(wq_loaded, 16)
            act.dma_start(bo_wide[:], bo.partition_broadcast(P).unsqueeze(1)).then_inc(bo_loaded, 16)

            for i in range(2):
                act.wait_ge(x_filled, i + 1)
                act.activation(normed_T[:, i * BANK:(i + 1) * BANK], x_bank[i][:], ACT.Copy).then_inc(x_drained, 1)

            def gate_sums(b):
                act.wait_ge(gate_max_ready, b + 1)
                for j in range(QT):
                    last = act.activation(exps[:, j, :], logits[:, j, :], ACT.Exp, bias=gate_neg_max[:, j:j + 1],
                                          accum_out=gate_sum[:, j:j + 1])
                last.then_inc(gate_sum_ready, 1)

            def attention(W, signals):
                HB = heads_a_bank(W)
                width = SK if W == SK else B * W

                def exponentials(n, r):
                    act.wait_ge(signals["max_ready"], 2 * n + r + 1)
                    if n >= 2:
                        act.wait_ge(signals["turn_filled"], 2 * (n - 2) + r + 1)
                    for i in range(HB):
                        c = slice(i * W, (i + 1) * W)
                        last = act.activation(probs[:, n % 2, r, c], score_bank[n % 2][r][:, c], ACT.Exp,
                                              bias=neg_max[:, n % 2, r, i:i + 1],
                                              accum_out=row_sum[:, n % 2, r, i:i + 1])
                    last.then_inc(signals["exp_done"], 1)

                def odd_heads(stage, bank, count):
                    act.wait_ge(signals["filled"], count)
                    act.wait_ge(zeros_ready, 3)
                    col = (FT if stage[0] == "k" else 2 * FT) + stage[1]
                    for i in range(BANK // width):
                        if W == SK:
                            to, from_ = kv_full[DH:P, stage[1], 1, :], bank[DH:P, :]
                        else:
                            to = (k_short if stage[0] == "k" else v_short)[DH:P, stage[1] + i, :, 1, :]
                            from_ = bank[DH:P, i * width:(i + 1) * width].rearrange("p (b k) -> p b k", b=B)
                        last = act.activation(to, from_, ACT.Identity, bias=bias_T[DH:P, col + i:col + i + 1])
                    last.then_inc(signals["odd_drained"], 1)

                count = 0
                for kind, at, *rest in steps(W):
                    if kind == "work":
                        count += 1
                        if at[0] in ("k", "v"):
                            odd_heads(at, rest[0], count)
                    elif kind == "exp":
                        exponentials(number(W, *at), rest[0])
                    elif kind == "logits":
                        gate_sums(at)

            act.wait_ge(flag_ready, 1)
            flag = act.value_load(short_flag[0:1, 0:1], min_val=0, max_val=1)
            with act.If(flag == 1):
                attention(TAIL, short)
            with act.Else():
                attention(SK, full)
            gate_sums(B - 1)

            def turned_rows(i):
                act.wait_ge(turned, i + 1)
                act.activation(rows_T[:, i * P:(i + 1) * P], banks[4 + i % 2][:, 0:P], ACT.Copy).then_inc(turn_drained, 1)

            def relu(i):
                act.wait_ge(hid_filled, i + 1)
                if i >= 2:
                    act.wait_ge(y_filled, i - 1)
                for c in range(HC):
                    act.activation(hidden[:, i % 2, c * P:(c + 1) * P], banks[i % 2][:, c * P:(c + 1) * P], ACT.Relu,
                                   bias=b1_stage[:, i % 3, c:c + 1]).then_inc(relu_done, 1)

            def relu_tile(i):
                if i + 1 < TILES:
                    turned_rows(i + 1)
                relu(i)

            act.wait_ge(table_ready, 1)
            used = act.value_load(used_tiles[0:1, 0:1], min_val=NT, max_val=TILES)
            turned_rows(0)
            for i in range(NT):
                relu_tile(i)
            for i in range(NT, TILES):
                with act.If(used > i):
                    relu_tile(i)

        @block.tensor
        def _(pe):
            def queries(bank, b, m0):
                for m in range(m0, m0 + 2):
                    last = pe.matmul(bank[:, (m - m0) * S:(m - m0 + 1) * S], wq_sb[:, m * P:(m + 1) * P],
                                     normed_T[:, b * S:(b + 1) * S], start=True, stop=True)
                return last

            pe.wait_ge(consts_made, 3)
            pe.wait_ge(biases_loaded, 64)
            pe.transpose(work_bank[:, 0:NB], bias_rows[:], ident[0:NB, 0:NB]).then_inc(bias_filled, 1)
            for i in range(2):
                pe.wait_ge(normed_ready, i + 1)
                for t in range(4):
                    last = pe.transpose(x_bank[i][:, t * P:(t + 1) * P], normed[:, i * 4 + t, :], ident[:])
                last.then_inc(x_filled, 1)
            pe.wait_ge(far_min_ready, 1)
            pe.matmul(out_bank[0:1, 0:1], far_min[:], ones[:, 0:1], start=True, stop=True).then_inc(flag_filled, 1)
            pe.wait_ge(wq_loaded, 16)
            for i in range(FT // 2):
                pe.wait_ge(x_drained, 1)
                queries(q0_bank[i], 0, 2 * i).then_inc(q0_filled, 1)
            pe.wait_ge(x_drained, 2)
            pe.wait_ge(bias_ready, 1)

            def transpose_rows(b):
                pe.wait_ge(h_ready, b + 1)
                for j in range(QT):
                    last = pe.transpose(work_bank[:, j * P:(j + 1) * P], normed2[:, j, :], ident[:])
                last.then_inc(router_filled, 1)

            def gate_logits(b):
                if b == 0:
                    pe.wait_ge(router_loaded, 32)
                pe.wait_ge(router_drained, 3 * b + 1)
                for j in range(QT):
                    last = pe.matmul(work_bank[:, j * E:(j + 1) * E], normed2_T[:, j * P:(j + 1) * P], wg_sb[:],
                                     start=True, stop=True)
                last.then_inc(router_filled, 1)

            def expert_ranks(b):
                if b == 0:
                    pe.wait_ge(more_consts, 10)
                pe.wait_ge(onehot_ready, b + 1)
                if b:
                    pe.wait_ge(seen_ready, b)
                for j in range(QT):
                    ranked = work_bank[:, j * E:(j + 1) * E]
                    pe.matmul(ranked, before[:], onehot[:, j, :], start=True, stop=False)
                    for i in range(j):
                        pe.matmul(ranked, ones_bf[:], onehot[:, i, :], start=False, stop=False)
                    last = pe.matmul(ranked, ones_bf[:], seen[:], start=False, stop=True)
                last.then_inc(router_filled, 1)

            def attention(W, signals):
                HB = heads_a_bank(W)
                width = SK if W == SK else B * W
                count = turns = odd = 0
                free_when = {}
                count_at = {}

                def claim(bank, *reads):
                    for signal, value in free_when.get(id(bank), ()):
                        pe.wait_ge(signal, value)
                    free_when[id(bank)] = reads

                def work(stage, bank):
                    nonlocal count, odd
                    count += 1
                    count_at[stage] = count
                    kv = stage[0] in ("k", "v")
                    odd += kv
                    claim(bank, (signals["drained"], count), *([(signals["odd_drained"], odd)] if kv else []))
                    if stage[0] == "ctx":
                        if W == SK:
                            pe.wait_ge(signals["ctx_loaded"], 16 * (stage[1] + 1))
                            for t in range(SK // P):
                                last = pe.transpose(bank[:, t * P:(t + 1) * P], ctx_all[:, t, :], ident[:])
                        else:
                            pe.wait_ge(tail_loaded, 32)
                            for t in range(2):
                                last = pe.transpose(bank[:, t * P:(t + 1) * P], ctx_tail[:, t, :], ident[:])
                    elif kv:
                        weights = wk_sb if stage[0] == "k" else wv_sb
                        if stage[1] == 0:
                            pe.wait_ge(wk_loaded if stage[0] == "k" else wv_loaded, 16)
                            pe.wait_ge(signals["drained"], max(n for s, n in count_at.items() if s[0] == "ctx"))
                        for i in range(BANK // width):
                            m = stage[1] + i
                            last = pe.matmul(bank[:, i * width:(i + 1) * width], weights[:, m * P:(m + 1) * P],
                                             ctx_T[:, 0:width], start=True, stop=True)
                    elif stage[0] == "q":
                        last = queries(bank, *stage[1:])
                    else:
                        _, b, c = stage
                        if c == 0:
                            pe.wait_ge(signals["drained"], max(n for s, n in count_at.items() if s[0] == "v"))
                            pe.wait_ge(signals["odd_drained"], odd)
                            if b == 0:
                                pe.wait_ge(wo_loaded, 16)
                        for k in range(4):
                            blk = c * 4 + k
                            if W == SK:
                                h, t = blk // (SK // P), blk % (SK // P)
                                m, values = h // 2, kv_full[:, h // 2, h % 2, t * P:(t + 1) * P]
                            else:
                                m, values = blk, v_short[:, blk, b, :, :].rearrange("p r k -> p (r k)")
                            last = pe.matmul(bank[:, k * D:(k + 1) * D], values, wo_sb[:, m, :], start=True, stop=True)
                    last.then_inc(signals["filled"], 1)

                def score(b, j, g):
                    n = number(W, b, j, g)
                    if n == 0:
                        pe.wait_ge(consts_made, 4)
                        pe.wait_ge(signals["mask_ready"], 1)
                    if g == 0 and j == 0:
                        if b == 0:
                            pe.wait_ge(q0_drained, FT // 2)
                        pe.wait_ge(signals["drained"], max(n for s, n in count_at.items() if s[0] == "k" or s[:2] == ("q", b)))
                        pe.wait_ge(signals["odd_drained"], odd)
                    for r in range(2):
                        bank = score_bank[n % 2][r]
                        if n >= 2:
                            pe.wait_ge(signals["exp_done"], 2 * (n - 2) + r + 1)
                        pe.matmul(bank[:], ident_bf[:], mask_bias[:, j, :], start=True, stop=False, skip_group_check=True)
                        if W == SK:
                            h = 2 * g + r
                            last = pe.matmul(bank[:], q_T[:, b % 2, h // 2, j * P:(j + 1) * P], kv_full[:, h // 2, h % 2, :],
                                             start=False, stop=True, skip_group_check=True)
                        else:
                            for i in range(HB // 2):
                                m = r * HB // 2 + i
                                last = pe.matmul(bank[:, i * 2 * W:(i + 1) * 2 * W], q_T[:, b % 2, m, j * P:(j + 1) * P],
                                                 k_short[:, m, b, :, :].rearrange("p r k -> p (r k)"),
                                                 start=False, stop=i == HB // 2 - 1, skip_group_check=True)
                        last.then_inc(signals["scored"], 1)

                def turn(b, j, g, r):
                    nonlocal turns
                    n = number(W, b, j, g)
                    turns += 1
                    claim(turn_bank[r], (signals["turn_drained"], turns))
                    pe.wait_ge(signals["normalised"], 2 * n + r + 1)
                    for k in range(4):
                        last = pe.transpose(turn_bank[r][:, k * P:(k + 1) * P], probs[:, n % 2, r, k * P:(k + 1) * P], ident[:])
                    last.then_inc(signals["turn_filled"], 1)

                def output(b, j, g):
                    if g == 0:
                        if b or j:
                            pe.wait_ge(x1_ready, b * QT + j)
                        if j == 0:
                            pe.wait_ge(signals["drained"], count_at["vo", b, 2 * groups(W) - 1])
                    base = 0 if W == SK else (b % 2) * 8
                    for r in range(2):
                        pe.wait_ge(signals["turn_drained"], turns - 1 + r)
                        for k in range(4):
                            first = g == 0 and r == 0 and k == 0
                            final = g == groups(W) - 1 and r == 1 and k == 3
                            last = pe.matmul(out_bank[:, 0:D], probs_T[:, r, k * P:(k + 1) * P],
                                             vo[:, base + (g * 2 + r) * 4 + k, :], start=first, stop=final)
                    last.then_inc(signals["out_filled"], 1)

                for kind, at, *rest in steps(W):
                    if kind == "work":
                        work(at, rest[0])
                    elif kind == "score":
                        score(*at)
                    elif kind == "turn":
                        turn(*at, rest[0])
                    elif kind == "out":
                        output(*at)
                    elif kind == "h_T":
                        claim(work_bank, (router_drained, 3 * at + 1))
                        transpose_rows(at)
                    elif kind == "logits":
                        claim(work_bank, (router_drained, 3 * at + 2))
                        gate_logits(at)
                    elif kind == "rank":
                        claim(work_bank, (router_drained, 3 * at + 3))
                        expert_ranks(at)

            pe.wait_ge(flag_ready, 1)
            flag = pe.value_load(short_flag[0:1, 0:1], min_val=0, max_val=1)
            with pe.If(flag == 1):
                attention(TAIL, short)
            with pe.Else():
                attention(SK, full)
            pe.wait_ge(router_drained, 3 * (B - 1))
            transpose_rows(B - 1)
            gate_logits(B - 1)
            pe.wait_ge(router_drained, 3 * (B - 1) + 2)
            expert_ranks(B - 1)
            pe.wait_ge(router_drained, 3 * B)
            pe.wait_ge(seen_ready, B)
            pe.matmul(work_bank[0:1, 0:E], ones_bf[:, 0:1], seen[:], start=True, stop=True).then_inc(router_filled, 1)

            def turn_rows(i):
                if i >= 2:
                    pe.wait_ge(turn_drained, i - 1)
                pe.wait_ge(slot_ready, i + 1)
                pe.transpose(banks[4 + i % 2][:, 0:P], slot_normed[:, i, :], ident[:]).then_inc(turned, 1)

            def hidden_tile(i):
                if i + 1 < TILES:
                    turn_rows(i + 1)
                pe.wait_ge(turn_drained, i + 1)
                pe.wait_ge(staged, i + 1)
                if i >= 2:
                    pe.wait_ge(relu_done, HC * (i - 1))
                for c in range(HC):
                    last = pe.matmul(banks[i % 2][:, c * P:(c + 1) * P], w1_stage[:, i % 3, c * P:(c + 1) * P],
                                     rows_T[:, i * P:(i + 1) * P], start=True, stop=True)
                last.then_inc(hid_filled, 1)

            def result_tile(i):
                e = pe.value_load(expert_of[0:1, i:i + 1], min_val=0, max_val=E - 1)
                if i >= 2:
                    pe.wait_ge(plus_ready, i - 1)
                for c in range(HC):
                    pe.wait_ge(relu_done, HC * i + c + 1)
                    last = pe.matmul(banks[2 + i % 2][:, 0:D].unsqueeze(1), hidden[:, i % 2, c * P:(c + 1) * P],
                                     w2_sb[:, bass.ds(e, 1), c * D:(c + 1) * D], start=(c == 0), stop=(c == HC - 1))
                last.then_inc(y_filled, 1)

            def from_tile(i):
                if i == TILES:
                    result_tile(i - 1)
                    return
                with pe.If(used > i):
                    hidden_tile(i)
                    result_tile(i - 1)
                    from_tile(i + 1)
                with pe.Else():
                    result_tile(i - 1)

            pe.wait_ge(table_ready, 1)
            pe.wait_ge(experts_loaded, 48)
            used = pe.value_load(used_tiles[0:1, 0:1], min_val=NT, max_val=TILES)
            turn_rows(0)
            hidden_tile(0)
            for i in range(1, NT):
                hidden_tile(i)
                result_tile(i - 1)
            from_tile(NT)

        @block.vector
        def _(dve):
            def chained(signal):
                links = 0

                def after(instruction):
                    nonlocal links
                    links += 1
                    instruction.then_inc(signal, 1)
                    dve.wait_ge(signal, links)
                return after

            after = chained(dve_done)

            dve.memset(zero_padded[:, FT * SK:FT * SK + DVE_ZEROS], 0.0).then_inc(zeros_ready, 1)
            x_flat = x_tok[:].rearrange("p b j d -> p (b j) d")
            dve.wait_ge(x_loaded, 16)
            for t in range(NT):
                last = dve.bn_stats(stats[:, t, :], x_flat[:, t, :])
            after(last)
            for t in range(NT):
                last = dve.bn_aggr(mean_var[:, t, :], stats[:, t, :])
            after(last)
            dve.tensor_scalar(var_eps[:], mean_var[:, :, 1], EPS, None, ALU.add).then_inc(var_ready, 1)

            dve.wait_ge(mask_loaded, 16)
            dve.tensor_reduce(far_min[:], mask_u8[:, :, 0:SK - TAIL], AX.XY, ALU.min).then_inc(far_min_ready, 1)
            dve.wait_ge(bias_filled, 1)
            dve.tensor_copy(bias_T[:], work_bank[:, 0:NB]).then_inc(bias_ready, 1)
            dve.wait_ge(rstd_ready, 1)
            for t in range(NT):
                last = dve.tensor_scalar(normed[:, t, :], x_flat[:, t, :], mean_var[:, t, 0:1], rstd[:, t:t + 1],
                                         ALU.subtract, ALU.mult)
                if t % 4 == 3:
                    last.then_inc(normed_ready, 1)
            dve.wait_ge(bias_ready, 1)
            dve.tensor_scalar(bq_scaled[:], bias_T[:, 0:FT], SCALE, None, ALU.mult).then_inc(bias_ready, 1)
            dve.wait_ge(flag_filled, 1)
            dve.tensor_scalar(short_flag[:], out_bank[0:1, 0:1], float(P), None, ALU.is_equal).then_inc(flag_ready, 1)

            def drain_queries(bank, b, m):
                bias = bq_scaled[:, m:m + 2].unsqueeze(2).to_broadcast([P, 2, S])
                return dve.scalar_tensor_tensor(out=q_T[:, b % 2, m:m + 2, :], in0=bank[:].rearrange("p (m s) -> p m s", s=S),
                                                scalar=SCALE, in1=bias, op0=ALU.mult, op1=ALU.add)

            dve.wait_ge(bias_ready, 2)
            for i in range(FT // 2):
                dve.wait_ge(q0_filled, i + 1)
                drain_queries(q0_bank[i], 0, 2 * i).then_inc(q0_drained, 1)

            def second_statistics(b):
                for j in range(QT):
                    dve.wait_ge(x1_ready, QT * b + j + 1)
                    last = dve.bn_stats(stats2[:, j, :], token_rows[:, QT * b + j, 0:D])
                return last

            def second_aggregate():
                for j in range(QT):
                    last = dve.bn_aggr(mean_var2[:, j, :], stats2[:, j, :])
                return last

            def second_variance():
                dve.tensor_scalar(var_eps2[:], mean_var2[:, :, 1], EPS, None, ALU.add).then_inc(var2_ready, 1)

            def second_normalise(b):
                dve.wait_ge(rstd2_ready, b + 1)
                if b:
                    dve.wait_ge(router_filled, 3 * (b - 1) + 1)
                for j in range(QT):
                    last = dve.tensor_scalar(normed2[:, j, :], token_rows[:, QT * b + j, 0:D], mean_var2[:, j, 0:1],
                                             rstd2[:, j:j + 1], ALU.subtract, ALU.mult)
                last.then_inc(h_ready, 1)
                dve.tensor_copy(token_rows[:, QT * b:QT * (b + 1), MEAN], mean_var2[:, :, 0])
                dve.tensor_copy(token_rows[:, QT * b:QT * (b + 1), RSTD], rstd2[:])

            def drain_normed(b):
                dve.wait_ge(router_filled, 3 * b + 1)
                dve.tensor_copy(normed2_T[:], work_bank[:, 0:S]).then_inc(router_drained, 1)

            def wide(column):
                return column.unsqueeze(2).to_broadcast([P, QT, E])

            def choose(b, after):
                if b == 0:
                    dve.wait_ge(more_consts, 10)
                    dve.wait_ge(router_loaded, 32)
                dve.wait_ge(router_filled, 3 * b + 2)
                dve.tensor_tensor(logits[:], work_bank[:, 0:QT * E].rearrange("p (j e) -> p j e", e=E),
                                  bg_wide[:].to_broadcast([P, QT, E]), ALU.add).then_inc(router_drained, 1)
                dve.wait_ge(router_drained, 3 * b + 2)
                dve.tensor_reduce(gate_neg_max[:], logits[:], AX.X, ALU.max, negate=True).then_inc(gate_max_ready, 1)
                dve.wait_ge(gate_max_ready, b + 1)
                after(dve.tensor_tensor(below_max[:], logits[:], wide(gate_neg_max[:]), ALU.add))
                after(dve.scalar_tensor_tensor(out=candidates[:], in0=below_max[:], scalar=0.0, in1=falling[:],
                                               op0=ALU.is_equal, op1=ALU.mult))
                after(dve.tensor_reduce(chosen[:], candidates[:], AX.X, ALU.max))
                dve.tensor_tensor(onehot[:], falling[:], wide(chosen[:]), ALU.is_equal).then_inc(onehot_ready, 1)
                dve.wait_ge(gate_sum_ready, b + 1)
                after(dve.reciprocal(token_rows[:, QT * b:QT * (b + 1), PROB], gate_sum[:]))

            def place(b, after):
                dve.wait_ge(router_filled, 3 * b + 3)
                dve.tensor_tensor(ranks[:], work_bank[:, 0:QT * E].rearrange("p (j e) -> p j e", e=E), onehot[:],
                                  ALU.mult).then_inc(router_drained, 1)
                dve.wait_ge(router_drained, 3 * b + 3)
                after(dve.tensor_reduce(rank[:], ranks[:], AX.X, ALU.add))
                dve.scalar_tensor_tensor(out=row_of[:, QT * b:QT * (b + 1)], in0=chosen[:], scalar=float(N), in1=rank[:],
                                         op0=ALU.mult, op1=ALU.add).then_inc(rows_ready, 1)
                after(dve.tensor_tensor(seen[:], seen[:], onehot[:, 0, :], ALU.add))
                dve.tensor_tensor(seen[:], seen[:], onehot[:, 1, :], ALU.add).then_inc(seen_ready, 1)

            def attention(W, signals):
                HB = heads_a_bank(W)
                width = SK if W == SK else B * W
                count = 0
                after = chained(signals["dve_done"])

                def work(stage, bank):
                    nonlocal count
                    count += 1
                    dve.wait_ge(signals["filled"], count)
                    if stage[0] == "ctx":
                        last = dve.tensor_copy(ctx_T[:, 0:width], bank[:, 0:width])
                    elif stage[0] in ("k", "v"):
                        if count == 2:
                            dve.wait_ge(zeros_ready, 3)
                        many = BANK // width
                        col = (FT if stage[0] == "k" else 2 * FT) + stage[1]
                        bias = bias_T[0:DH, col:col + many].unsqueeze(2).to_broadcast([DH, many, width])
                        if W == SK:
                            to = kv_full[0:DH, stage[1]:stage[1] + 1, 0, :]
                        else:
                            to = (k_short if stage[0] == "k" else v_short)[0:DH, stage[1]:stage[1] + many, :, 0, :]
                            to = to.rearrange("p m b k -> p (m b) k")
                        from_ = bank[0:DH, :].rearrange("p (m s) -> p m s", s=width)
                        if W != SK:
                            from_ = bank[0:DH, :].rearrange("p (m k) -> p m k", k=W)
                            bias = bias_T[0:DH, col:col + many].unsqueeze(2).unsqueeze(3).to_broadcast([DH, many, B, W])
                            to = to.rearrange("p (m b) k -> p m b k", b=B)
                            from_ = from_.rearrange("p (m b) k -> p m b k", b=B)
                        last = dve.tensor_tensor(to, from_, bias, ALU.add)
                    elif stage[0] == "q":
                        last = drain_queries(bank, *stage[1:])
                    else:
                        _, b, c = stage
                        base = (0 if W == SK else (b % 2) * 8) + c * 4
                        last = dve.tensor_copy(vo[:, base:base + 4, :], bank[:].rearrange("p (k d) -> p k d", d=D))
                    last.then_inc(signals["drained"], 1)

                turns = 0
                for kind, at, *rest in steps(W):
                    if kind == "work":
                        work(at, rest[0])
                    elif kind == "score":
                        n = number(W, *at)
                        for r in range(2):
                            dve.wait_ge(signals["scored"], 2 * n + r + 1)
                            dve.tensor_reduce(neg_max[:, n % 2, r, 0:HB],
                                              score_bank[n % 2][r][:].rearrange("p (h w) -> p h w", w=W),
                                              AX.X, ALU.max, negate=True).then_inc(signals["max_ready"], 1)
                        if n == 0:
                            after(dve.tensor_reduce(row_min[:], mask_u8[:], AX.X, ALU.min))
                            after(dve.tensor_scalar(blown[:], row_min[:], HUGE, HUGE, ALU.mult, ALU.mult))
                            after(dve.tensor_tensor(dead_row[:], blown[:], blown[:], ALU.subtract))
                    elif kind == "turn":
                        turns += 1
                        dve.wait_ge(signals["turn_filled"], turns)
                        dve.tensor_copy(probs_T[:, rest[0], :], turn_bank[rest[0]][:]).then_inc(signals["turn_drained"], 1)
                    elif kind == "inverse":
                        n, r = number(W, *at), rest[0]
                        dve.wait_ge(signals["exp_done"], 2 * n + r + 1)
                        dve.reciprocal(inv_sum[:, n % 2, r, 0:HB], row_sum[:, n % 2, r, 0:HB]).then_inc(signals["inv_ready"], 1)
                    elif kind == "out":
                        b, j, g = at
                        if g == groups(W) - 1:
                            if b == 0 and j == 0:
                                dve.wait_ge(x_bo_ready, 1)
                            dve.wait_ge(signals["out_filled"], number(W, *at) + 1)
                            dve.scalar_tensor_tensor(out=token_rows[:, b * QT + j, 0:D], in0=out_bank[:, 0:D],
                                                     scalar=dead_row[:, j:j + 1], in1=x_bo[:, b * QT + j, :],
                                                     op0=ALU.add, op1=ALU.add).then_inc(x1_ready, 1)
                    elif kind == "ln2":
                        after(second_statistics(at))
                        after(second_aggregate())
                        second_variance()
                    elif kind == "normalise":
                        second_normalise(at)
                    elif kind == "h_T":
                        drain_normed(at)
                    elif kind == "logits":
                        choose(at, after)
                    elif kind == "rank":
                        place(at, after)

            dve.wait_ge(flag_ready, 1)
            flag = dve.value_load(short_flag[0:1, 0:1], min_val=0, max_val=1)
            with dve.If(flag == 1):
                attention(TAIL, short)
            with dve.Else():
                attention(SK, full)
            after(second_statistics(B - 1))
            after(second_aggregate())
            second_variance()
            second_normalise(B - 1)
            drain_normed(B - 1)
            choose(B - 1, after)
            place(B - 1, after)

            dve.wait_ge(router_filled, 3 * B + 1)
            after(dve.tensor_copy(counts[:], work_bank[0:1, 0:E]))
            after(dve.tensor_tensor(pairs[:], counts[:].unsqueeze(2).to_broadcast([1, E, E]), thresholds[:], ALU.is_gt))
            after(dve.tensor_reduce(tiles_of[:], pairs[:], AX.X, ALU.add))
            after(dve.tensor_tensor(pairs[:], tiles_of[:].unsqueeze(1).to_broadcast([1, E, E]), upto[:], ALU.mult))
            after(dve.tensor_reduce(end_of[:], pairs[:], AX.X, ALU.add))
            after(dve.tensor_tensor(passed[:], tile_index[:], end_of[:].unsqueeze(1).to_broadcast([1, TILES, E]), ALU.is_ge))
            dve.tensor_copy(used_tiles[:], end_of[:, E - 1:E])
            after(dve.tensor_tensor(passed_tiles[:], passed[:], tiles_of[:].unsqueeze(1).to_broadcast([1, TILES, E]), ALU.mult))
            dve.tensor_reduce(expert_f[:], passed[:], AX.X, ALU.add)
            after(dve.tensor_reduce(first_f[:], passed_tiles[:], AX.X, ALU.add))
            after(dve.scalar_tensor_tensor(out=row_f[:], in0=expert_f[:], scalar=-float(N), in1=tile_row[:], op0=ALU.mult, op1=ALU.add))
            dve.tensor_scalar(expert_of[:], expert_f[:], float(E - 1), None, ALU.min)
            dve.scalar_tensor_tensor(out=first_row[:], in0=first_f[:], scalar=-float(P), in1=row_f[:], op0=ALU.mult,
                                     op1=ALU.add).then_inc(table_ready, 1)

            dve.wait_ge(table_ready, 1)
            dve.wait_ge(experts_loaded, 48)

            def normalise_slots(i):
                dve.wait_ge(tile_loaded[i], 16)
                dve.tensor_scalar(slot_normed[:, i, :], tile_rows[:, i, 0:D], tile_rows[:, i, MEAN:MEAN + 1],
                                  tile_rows[:, i, RSTD:RSTD + 1], ALU.subtract, ALU.mult).then_inc(slot_ready, 1)

            def stage_weights(i):
                e = dve.value_load(expert_of[0:1, i:i + 1], min_val=0, max_val=E - 1)
                if i >= 3:
                    dve.wait_ge(relu_done, HC * (i - 2))
                dve.tensor_copy(b1_stage[:, i % 3, :].unsqueeze(1),
                                bias_T[:, 3 * FT:NB].rearrange("p (e c) -> p e c", c=HC)[:, bass.ds(e, 1), :])
                dve.tensor_copy(w1_stage[:, i % 3, :].unsqueeze(1), w1_sb[:, bass.ds(e, 1), :]).then_inc(staged, 1)
                return e

            def finish_tile(i, e):
                dve.wait_ge(y_filled, i + 1)
                dve.tensor_tensor(plus_b2[:, i % 2, :].unsqueeze(1), banks[2 + i % 2][:, 0:D].unsqueeze(1),
                                  b2_wide[:, bass.ds(e, 1), :], ALU.add).then_inc(plus_ready, 1)
                dve.wait_ge(plus_ready, i + 1)
                dve.scalar_tensor_tensor(out=results[:, i, :], in0=plus_b2[:, i % 2, :], scalar=tile_rows[:, i, PROB:PROB + 1],
                                         in1=tile_rows[:, i, 0:D], op0=ALU.mult, op1=ALU.add).then_inc(result_ready, 1)

            def prepare_after(i):
                if i + 2 < TILES:
                    normalise_slots(i + 2)
                return stage_weights(i + 1) if i + 1 < TILES else None

            def from_tile(i, before_e, e):
                if i == TILES:
                    finish_tile(i - 1, before_e)
                    return
                with dve.If(used > i):
                    next_e = prepare_after(i)
                    finish_tile(i - 1, before_e)
                    from_tile(i + 1, e, next_e)
                with dve.Else():
                    finish_tile(i - 1, before_e)

            used = dve.value_load(used_tiles[0:1, 0:1], min_val=NT, max_val=TILES)
            before_e = None
            e = stage_weights(0)
            normalise_slots(0)
            normalise_slots(1)
            for i in range(NT):
                next_e = prepare_after(i)
                if i:
                    finish_tile(i - 1, before_e)
                before_e, e = e, next_e
            from_tile(NT, before_e, e)


_INS = ["x", "ctx_1024", "mask_1xSxS2_bk1", "L0_xattn_Wq", "L0_xattn_bq", "L0_xattn_Wk", "L0_xattn_bk",
        "L0_xattn_Wv", "L0_xattn_bv", "L0_xattn_Wo", "L0_xattn_bo", "L0_ffn_w_gate", "L0_ffn_b_gate",
        "L0_ffn_W1", "L0_ffn_b1", "L0_ffn_W2", "L0_ffn_b2"]


def kernel(**inputs):
    import numpy as np
    import concourse.bacc as bacc
    from concourse import mybir as _mybir
    from concourse.bass_utils import run_bass_kernel_spmd

    nc = bacc.Bacc("TRN2", target_bir_lowering=False, num_devices=1)
    arrays, args = {}, []
    for name in _INS:
        a = np.ascontiguousarray(inputs[name])
        arrays[f"in_{name}"] = a
        args.append(nc.dram_tensor(f"in_{name}", a.shape, _mybir.dt.from_np(a.dtype), kind="ExternalInput").ap())
    shape = arrays["in_x"].shape
    args.append(nc.dram_tensor("out_x", shape, _mybir.dt.float32, kind="ExternalOutput").ap())
    xattn_moe(nc, *args)
    r = run_bass_kernel_spmd(nc, [arrays], core_ids=[0])
    return np.asarray(r.results[0]["out_x"])
```

```python
from contextlib import ExitStack

import concourse.bass as bass
from concourse import mybir
from concourse.alu_op_type import AluOpType as ALU

ACT = mybir.ActivationFunctionType
AX = mybir.AxisListType
F32 = mybir.dt.float32
BF16 = mybir.dt.bfloat16
I32 = mybir.dt.int32
U8 = mybir.dt.uint8

P = 128
BANK = 512
TAIL = 64
MASKED = -1e30
HUGE = 3e38
EPS = 1e-5



def xattn_moe(nc, x, ctx_in, mask, Wq, bq, Wk, bk, Wv, bv, Wo, bo,
              w_gate, b_gate, W1, b1, W2, b2, out):
    B, S, D = x.shape
    SK = ctx_in.shape[1]
    HD = Wq.shape[1]
    DH = 64
    H = HD // DH
    E = w_gate.shape[1]
    F = W1.shape[2]
    QT = S // P
    NT = B * QT
    N = NT * P
    FT = HD // P
    HC = F // P
    SCALE = DH ** -0.5
    MEAN, RSTD, PROB, INDEX = D, D + 1, D + 2, D + 3
    ROW = D + 4
    TILES = NT + E - 1
    EARLY_BATCHES = B - 2
    EARLY = 3
    ALL = EARLY + TILES
    ROUTED = [[QT * b + j for j in range(QT)] for b in range(B - 1)] + [[QT * (B - 1) + j] for j in range(QT)]
    SPARE = TILES - NT
    DVE_ZEROS = FT * SK * 5 // 8
    assert EARLY <= EARLY_BATCHES * QT <= NT - EARLY and D == P and FT * 2 == H and QT == 2 and F == BANK and SPARE * P <= N

    with ExitStack() as stack:
        def sb(name, shape, dt=F32):
            return stack.enter_context(nc.sbuf_tensor(name, shape, dt))

        def sem(name):
            return stack.enter_context(nc.semaphore(name))

        banks = [stack.enter_context(nc.psum_tensor(f"bank{i}", [P, BANK], F32)) for i in range(8)]
        score_bank = [[banks[0], banks[1]], [banks[2], banks[3]]]
        turn_bank = [banks[4], banks[5]]
        work_bank = banks[6]
        out_bank = banks[7]
        x_bank = turn_bank
        q0_bank = banks[0:3]
        tail_bank = banks[3]

        def normed2_bank(k):
            return work_bank if k < B - 1 else banks[1]

        def ranks_bank(k):
            return work_bank if k < B - 1 else banks[3]

        x_tok = sb("x_tok", [P, B, QT, D])
        mask_u8 = sb("mask_u8", [P, QT, SK], U8)
        ctx_tail = sb("ctx_tail", [P, 2, D])
        ctx_all = sb("ctx_all", [P, SK // P, D])
        wq_sb = sb("wq_sb", [P, HD])
        wk_sb = sb("wk_sb", [P, HD])
        wv_sb = sb("wv_sb", [P, HD])
        wo_sb = sb("wo_sb", [P, FT, D])
        bo_wide = sb("bo_wide", [P, 1, D])
        NB = 3 * FT + E * HC
        bias_rows = sb("bias_rows", [NB, P])
        wg_sb = sb("wg_sb", [P, E])
        bg_wide = sb("bg_wide", [P, 1, E])
        w1_sb = sb("w1_sb", [P, E, F])
        w2_sb = sb("w2_sb", [P, E, HC * D])
        b2_wide = sb("b2_wide", [P, E, D])

        ident = sb("ident", [P, P])
        ident_bf = sb("ident_bf", [P, P], BF16)
        ones = sb("ones", [P, P])
        ones_bf = sb("ones_bf", [P, P], BF16)
        before = sb("before", [P, P], BF16)
        minus_half = sb("minus_half", [P, NT])
        falling = sb("falling", [P, QT, E])
        thresholds = sb("thresholds", [1, E, E])
        upto = sb("upto", [1, E, E])
        full_at = sb("full_at", [1, E, E])
        tile_index = sb("tile_index", [1, TILES, E])
        tile_row = sb("tile_row", [1, TILES])
        empty_row = sb("empty_row", [P, 1, ROW])

        stats = sb("stats", [P, NT, nc.vector.BN_STATS_DIM])
        mean_var = sb("mean_var", [P, NT, nc.vector.BN_AGGR_DIM])
        var_eps = sb("var_eps", [P, NT])
        rstd = sb("rstd", [P, NT])
        normed = sb("normed", [P, NT, D])
        normed_T = sb("normed_T", [P, N])
        x_bo = sb("x_bo", [P, NT, D])
        bias_T = sb("bias_T", [P, NB])
        bq_scaled = sb("bq_scaled", [P, FT])
        row_min = sb("row_min", [P, QT])
        far_min = sb("far_min", [P, 1])
        blown = sb("blown", [P, QT])
        dead_row = sb("dead_row", [P, QT])
        short_flag = sb("short_flag", [1, 1], I32)

        mask_bias = sb("mask_bias", [P, QT, BANK], BF16)
        ctx_T = sb("ctx_T", [P, BANK])
        q_T = sb("q_T", [P, 2, FT, S])
        zero_padded = sb("zero_padded", [P, FT * 2 * SK])
        k_short, v_short = (zero_padded[:, i * FT * B * 2 * TAIL:(i + 1) * FT * B * 2 * TAIL].rearrange(
            "p (m b r k) -> p m b r k", m=FT, b=B, r=2) for i in range(2))
        kv_full = zero_padded[:].rearrange("p (m r k) -> p m r k", m=FT, r=2)
        VO_BLOCKS = H * SK // P
        vo = sb("vo", [P, VO_BLOCKS, D])
        neg_max = sb("neg_max", [P, 2, 2, 8])
        row_sum = sb("row_sum", [P, 2, 2, 8])
        inv_sum = sb("inv_sum", [P, 2, 2, 8])
        probs = sb("probs", [P, 2, 2, BANK])
        probs_T = sb("probs_T", [P, 2, BANK])

        stats2 = sb("stats2", [P, QT, nc.vector.BN_STATS_DIM])
        mean_var2 = sb("mean_var2", [P, QT, nc.vector.BN_AGGR_DIM])
        var_eps2 = sb("var_eps2", [P, QT])
        rstd2 = sb("rstd2", [P, QT])
        token_rows = sb("token_rows", [P, NT, ROW])
        normed2 = sb("normed2", [P, QT, D])
        normed2_T = sb("normed2_T", [P, S])
        logits = sb("logits", [P, QT, E])
        exps = sb("exps", [P, QT, E])
        gate_max = sb("gate_max", [P, QT])
        gate_neg_max = sb("gate_neg_max", [P, QT])
        gate_sum = sb("gate_sum", [P, QT])
        candidates = sb("candidates", [P, QT, E])
        chosen = sb("chosen", [P, QT])
        onehot = sb("onehot", [P, QT, E], BF16)
        seen = sb("seen", [P, E], BF16)
        ranks = sb("ranks", [P, QT, E])
        rank = sb("rank", [P, QT])
        row_of = sb("row_of", [P, NT], I32)

        pairs = sb("pairs", [1, E, E])
        early_counts = sb("early_counts", [1, E])
        full_of = sb("full_of", [1, E])
        end_full = sb("end_full", [1, E])
        end_early = sb("end_early", [1, 1 + E])
        early_of = sb("early_of", [1, E + 1])
        early_step = sb("early_step", [1, E])
        early_row_step = sb("early_row_step", [1, E])
        late_row_base = sb("late_row_base", [1, E])
        late_row_step = sb("late_row_step", [1, E])
        late_tile_row = sb("late_tile_row", [1, TILES])
        late_thresholds = sb("late_thresholds", [1, E, E])
        late_of = sb("late_of", [1, E])
        end_of = sb("end_of", [1, E])
        passed = sb("passed", [1, TILES, E])
        passed_rows = sb("passed_rows", [1, TILES, E])
        expert_f = sb("expert_f", [1, TILES])
        row_f = sb("row_f", [1, TILES])
        expert_of = sb("expert_of", [1, ALL], I32)
        first_row = sb("first_row", [1, ALL], I32)
        used_tiles = sb("used_tiles", [1, 1], I32)

        assert VO_BLOCKS * D >= TILES * (ROW + P + 2 * D) + 2 * D and FT * 2 * SK >= 5 * F + EARLY * D
        flat = vo[:].rearrange("p t d -> p (t d)")
        tile_rows = flat[:, 0:TILES * ROW].rearrange("p (t d) -> p t d", d=ROW)
        rows_T = flat[:, TILES * ROW:TILES * (ROW + P)]
        slot_normed = flat[:, TILES * (ROW + P):TILES * (ROW + P + D)].rearrange("p (t d) -> p t d", d=D)
        plus_b2 = flat[:, TILES * (ROW + P + 2 * D):TILES * (ROW + P + 2 * D) + 2 * D].rearrange("p (t d) -> p t d", d=D)
        results = flat[:, TILES * (ROW + P + D):TILES * (ROW + P + 2 * D)].rearrange("p (t d) -> p t d", d=D)
        w1_stage = zero_padded[:, 0:3 * F].rearrange("p (i f) -> p i f", i=3)
        hidden = zero_padded[:, 3 * F:5 * F].rearrange("p (i f) -> p i f", i=2)
        results_early = zero_padded[:, 5 * F:5 * F + EARLY * D].rearrange("p (t d) -> p t d", d=D)
        b1_stage = sb("b1_stage", [P, 3, HC])
        token_of = sb("token_of", [P, ALL], I32)
        tile_rows_early = sb("tile_rows_early", [P, EARLY, ROW])
        slot_normed_early = sb("slot_normed_early", [P, EARLY, D])
        b2_early = sb("b2_early", [P, EARLY, D])
        rows_T_early = sb("rows_T_early", [P, EARLY * P])

        def rows_at(i, columns):
            return tile_rows_early[:, i, columns] if i < EARLY else tile_rows[:, i - EARLY, columns]

        def slot_normed_at(i):
            return slot_normed_early[:, i, :] if i < EARLY else slot_normed[:, i - EARLY, :]

        def rows_T_at(i):
            return rows_T_early[:, i * P:(i + 1) * P] if i < EARLY else rows_T[:, (i - EARLY) * P:(i - EARLY + 1) * P]

        def results_at(i):
            return results_early[:, i, :] if i < EARLY else results[:, i - EARLY, :]

        out_rows = out.rearrange("b s d -> (b s) d")
        regions = nc.dram_tensor("regions", [(E + 1) * N, ROW], F32).ap()

        x_loaded = [sem("x_loaded0"), sem("x_loaded1")]
        mask_loaded, tail_loaded, biases_loaded = map(sem, ("mask_loaded", "tail_loaded", "biases_loaded"))
        wq_loaded, wk_loaded, wv_loaded, wo_loaded, bo_loaded = map(sem, ("wq_loaded", "wk_loaded", "wv_loaded", "wo_loaded", "bo_loaded"))
        router_loaded, experts_loaded = sem("router_loaded"), sem("experts_loaded")
        cleared, consts_made, more_consts = sem("cleared"), sem("consts_made"), sem("more_consts")
        var_ready, rstd_ready, normed_ready, x_bo_ready = map(sem, ("var_ready", "rstd_ready", "normed_ready", "x_bo_ready"))
        tail_filled, tail_drained = sem("tail_filled"), sem("tail_drained")
        bias_filled, bias_ready, flag_filled = sem("bias_filled"), sem("bias_ready"), sem("flag_filled")
        x_filled, x_drained, q0_filled, q0_drained = map(sem, ("x_filled", "x_drained", "q0_filled", "q0_drained"))
        far_min_ready, flag_ready, zeros_ready = sem("far_min_ready"), sem("flag_ready"), sem("zeros_ready")
        dve_done = sem("dve_done")
        x1_ready = sem("x1_ready")
        var2_ready, rstd2_ready, h_ready = sem("var2_ready"), sem("rstd2_ready"), sem("h_ready")
        normed2_filled, normed2_drained, logits_filled, logits_drained, ranks_filled, ranks_drained = map(
            sem, ("normed2_filled", "normed2_drained", "logits_filled", "logits_drained", "ranks_filled", "ranks_drained"))
        gate_max_ready, gate_sum_ready = sem("gate_max_ready"), sem("gate_sum_ready")
        counts_filled = sem("counts_filled")
        onehot_ready, seen_ready, rows_ready, table_ready = map(sem, ("onehot_ready", "seen_ready", "rows_ready", "table_ready"))
        regions_cleared, scattered_early, scattered = sem("regions_cleared"), sem("scattered_early"), sem("scattered")
        early_counts_filled, early_table_ready, early_staged = map(
            sem, ("early_counts_filled", "early_table_ready", "early_staged"))
        early_counts_ready = sem("early_counts_ready")
        tile_loaded = [sem(f"tile_loaded{i}") for i in range(ALL)]
        slot_ready, turned, turn_drained = sem("slot_ready"), sem("turned"), sem("turn_drained")
        staged, hid_filled, relu_done = sem("staged"), sem("hid_filled"), sem("relu_done")
        y_filled, plus_ready, result_ready, result_scattered = map(sem, ("y_filled", "plus_ready", "result_ready", "result_scattered"))
        tokens_ready = sem("tokens_ready")

        def semaphores(name):
            return {signal: sem(f"{name}_{signal}") for signal in (
                "ctx_loaded", "mask_ready", "filled", "drained", "odd_drained", "scored", "max_ready",
                "exp_done", "inv_ready", "normalised", "turn_filled", "turn_drained", "out_filled", "centered", "wide_normalised", "dve_done")}

        short, full = semaphores("short"), semaphores("full")

        def heads_a_bank(W):
            return BANK // W

        def odd_on_scalar(stage):
            return stage[0] in ("k", "v")

        def groups(W):
            return H // 2 // heads_a_bank(W)

        def number(W, b, j, g):
            return (b * QT + j) * groups(W) + g

        def steps(W):
            rotation = [work_bank, turn_bank[0], turn_bank[1]]
            turn = 0

            def rotating(stages):
                nonlocal turn
                for stage in stages:
                    yield "work", stage, rotation[turn % 3]
                    turn += 1

            keys = [("k", m) for m in range(0, FT, 1 if W == SK else 2)]
            values = [("v", m) for m in range(0, FT, 1 if W == SK else 2)]
            held = None
            for b in range(B):
                room = []
                if W == SK:
                    yield from rotating([("ctx", b)] + values + [("vo", b, c) for c in range(2 * groups(W))] + keys)
                    yield from rotating([("q", b, m) for m in range(0, FT, 2)][-1 if b == 0 else 0:])
                elif b == 0:
                    yield from rotating(keys + [("q", 0, FT - 2), ("q", 1, 0)])
                else:
                    room = [("vo", b, 0), ("vo", b, 1)] + [("q", b + 1, m) for m in range(0, FT, 2) if b + 1 < B]
                for j in range(QT):
                    for g in range(groups(W)):
                        now = (b, j, g)
                        yield "score", now
                        if W != SK and b == 0 and j == 1:
                            yield from rotating([("q", 1, 4)] + values + [("q", 1, 6), ("vo", 0, 0), ("vo", 0, 1)])
                        spread = W != SK and b == B - 1 and j == 1
                        yield "exp", now, 0
                        yield ("wide_exp" if spread else "exp"), now, 1
                        if W != SK and b == 0 and j == 0:
                            yield from rotating([("q", 1, 2)])
                            yield "inverse", now, 0
                            yield "inverse", now, 1
                            held = now
                            continue
                        if g == 0 and j == 0 and b == B - 1:
                            yield "early_counts", b
                        if held:
                            yield "turn", held, 0
                            yield "turn", held, 1
                        if spread:
                            yield "center", now
                        if g == 0 and j == 1 and b >= 1:
                            yield "normalise", b - 1
                        if room:
                            yield "work", room.pop(0), work_bank
                        yield "inverse", now, 0
                        if g == 0 and j == 0 and b == B - 1:
                            yield "early_table", b
                        if held:
                            yield "out", held, 0
                            yield "out", held, 1
                        yield ("wide_normalise" if spread else "inverse"), now, 1
                        if g == 0 and j == 1 and b >= 1:
                            yield "h_T", b - 1
                        if g == 0 and j == 0 and b >= 2:
                            yield "rank", b - 2
                        if room:
                            yield "work", room.pop(0), turn_bank[0]
                        if g == 0 and j == 0 and b >= 1 and W != SK:
                            yield "ln2", b - 1
                        if spread:
                            yield "warm_up", 4, banks[0]
                        if g == 0 and j == 1 and b == B - 1:
                            yield "ln2", b
                        if room:
                            yield "work", room.pop(0), turn_bank[1]
                        if g == 0 and j == 1 and 1 <= b < B - 1:
                            yield "logits", b - 1
                        if g == 0 and j == 0 and b >= 2:
                            yield "scatter", b - 2
                        held = now
                if b == B - 1:
                    yield "last_turn", held, 0
                    yield "last_turn", held, 1
                    yield "logits", b - 1
                    yield "out", held, 0
                    yield "early_slots", 0
                    yield "early_slots", 1
                    yield "late_constants", b
                    yield "out", held, 1
                    yield "warm_up", 3, banks[2]
                    yield "early_turn", 0
                    yield "early_stage", 0
                    yield "normalise", b
                    yield "ln2", B
                    yield "h_T", b
                    yield "rank", b - 1
                    yield "warm_up", 2, banks[2]
                    yield "normalise", B
                    yield "logits", b
                    yield "early_hidden", 0
                    yield "early_turn", 1
                    yield "early_stage", 1
                    yield "h_T", B
                    yield "warm_up", 2, banks[2]
                    yield "rank", b
                    yield "scatter", b - 1
                    yield "scatter", b
                    yield "logits", B
                    yield "warm_up", 5, banks[2]
                    yield "early_slots", 2
                    yield "rank", B
                    yield "warm_up", 2, banks[2]
                    yield "scatter", B
                elif W == SK:
                    yield "turn", held, 0
                    yield "turn", held, 1
                    yield "out", held, 0
                    yield "out", held, 1
                    yield "ln2", b
                    held = None

        def work_until(W, stage):
            count = 0
            for kind, at, *_ in steps(W):
                count += kind == "work"
                if kind == "work" and at == stage:
                    return count

        block = stack.enter_context(nc.Block())

        @block.sync
        def _(sp):
            for i in range(2):
                sp.dma_start(x_tok[:, 2 * i:2 * i + 2, :, :],
                             x.rearrange("b (p j) d -> p b j d", j=QT)[:, 2 * i:2 * i + 2, :, :]).then_inc(x_loaded[i], 16)
            sp.dma_start(mask_u8[:], mask[0].rearrange("(p j) k -> p j k", j=QT)).then_inc(mask_loaded, 16)
            for r in range(2):
                sp.dma_start(ctx_tail[r * TAIL:(r + 1) * TAIL, :, :],
                             ctx_in.rearrange("(c r) k d -> r k c d", r=2)[r, SK - TAIL:SK, :, :]).then_inc(tail_loaded, 16)
            sp.dma_start(wk_sb[:], Wk).then_inc(wk_loaded, 16)
            sp.dma_start(wv_sb[:], Wv).then_inc(wv_loaded, 16)
            sp.dma_start(wo_sb[:], Wo.rearrange("(m p) d -> p m d", p=P)).then_inc(wo_loaded, 16)
            sp.dma_start(wg_sb[:], w_gate).then_inc(router_loaded, 16)
            sp.dma_start(bg_wide[:], b_gate.partition_broadcast(P).unsqueeze(1)).then_inc(router_loaded, 16)
            sp.wait_ge(more_consts, 2)
            sp.dma_start(regions[0:SPARE * P, :].rearrange("(t p) d -> p t d", p=P),
                         empty_row[:].to_broadcast([P, SPARE, ROW])).then_inc(regions_cleared, 16)
            sp.dma_start(regions[N:(E + 1) * N, :].rearrange("(t p) d -> p t d", p=P),
                         empty_row[:].to_broadcast([P, E * NT, ROW])).then_inc(regions_cleared, 16)
            sp.dma_start(w1_sb[:], W1.rearrange("e d f -> d e f")).then_inc(experts_loaded, 16)
            sp.dma_start(w2_sb[:].rearrange("p e (c d) -> p e c d", d=D),
                         W2.rearrange("e (c p) d -> p e c d", p=P)).then_inc(experts_loaded, 16)
            sp.dma_start(b2_wide[:], b2.partition_broadcast(P)).then_inc(experts_loaded, 16)
            sp.wait_ge(flag_ready, 1)
            flag = sp.value_load(short_flag[0:1, 0:1], min_val=0, max_val=1)
            with sp.If(flag == 0):
                for b in range(B):
                    if b:
                        sp.wait_ge(full["drained"], work_until(SK, ("ctx", b - 1)))
                    sp.dma_start(ctx_all[:], ctx_in[b].rearrange("(t p) d -> p t d", p=P)).then_inc(full["ctx_loaded"], 16)
            sp.wait_ge(early_table_ready, 1)
            sp.wait_ge(scattered_early, 16 * EARLY_BATCHES * QT)
            for i in range(EARLY):
                row = sp.value_load(first_row[0:1, i:i + 1], min_val=0, max_val=(E + 1) * N - P)
                sp.dma_start(rows_at(i, slice(0, ROW)), regions[bass.ds(row, P), :]).then_inc(tile_loaded[i], 16)
            sp.wait_ge(table_ready, 1)
            rows = [sp.value_load(first_row[0:1, i:i + 1], min_val=0, max_val=(E + 1) * N - P) for i in (EARLY, EARLY + 1)]
            sp.wait_ge(scattered, 16 * (NT - EARLY_BATCHES * QT))
            for i in range(EARLY, ALL):
                row = rows[i - EARLY] if i < EARLY + 2 else sp.value_load(first_row[0:1, i:i + 1], min_val=0,
                                                                          max_val=(E + 1) * N - P)
                sp.dma_start(rows_at(i, slice(0, ROW)), regions[bass.ds(row, P), :]).then_inc(tile_loaded[i], 16)
            for i in range(NT, ALL):
                sp.wait_ge(tile_loaded[i], 16)

        @block.gpsimd
        def _(pool):
            pool.memset(ident[:], 0.0).then_inc(cleared, 1)
            pool.memset(ones[:], 1.0).then_inc(consts_made, 1)
            pool.memset(minus_half[:], -0.5).then_inc(consts_made, 1)
            pool.wait_ge(cleared, 1)
            pool.affine_select(out=ident[:], in_=ident[:], compare_op=ALU.not_equal, fill=1.0, base=0,
                               pattern=[[-1, P]], channel_multiplier=1).then_inc(consts_made, 1)
            pool.memset(zero_padded[:, 0:FT * SK], 0.0).then_inc(zeros_ready, 1)

            pool.wait_ge(consts_made, 3)
            for i in range(2):
                c = slice(i * NT // 2, (i + 1) * NT // 2)
                pool.wait_ge(var_ready, i + 1)
                pool.tensor_tensor(rstd[:, c], var_eps[:, c], minus_half[:, c], ALU.pow).then_inc(rstd_ready, 1)
            pool.tensor_copy(ident_bf[:], ident[:]).then_inc(consts_made, 1)
            pool.memset(zero_padded[:, FT * SK + DVE_ZEROS:2 * FT * SK], 0.0).then_inc(zeros_ready, 1)

            pool.memset(empty_row[:], 0.0).then_inc(cleared, 1)
            pool.memset(ones_bf[:], 1.0).then_inc(more_consts, 1)
            pool.wait_ge(cleared, 2)
            pool.memset(empty_row[:, :, INDEX], float(N)).then_inc(more_consts, 1)
            pool.iota(falling[:], [[0, QT], [-1, E]], base=E, channel_multiplier=0,
                      allow_small_or_imprecise_dtypes=True).then_inc(more_consts, 1)
            pool.iota(thresholds[:], [[0, E], [P, E]], base=0, channel_multiplier=0,
                      allow_small_or_imprecise_dtypes=True).then_inc(more_consts, 1)
            pool.iota(full_at[:], [[0, E], [P, E]], base=P, channel_multiplier=0,
                      allow_small_or_imprecise_dtypes=True).then_inc(more_consts, 1)
            pool.memset(early_of[:], 0.0).then_inc(more_consts, 1)
            pool.memset(end_early[:], 0.0).then_inc(more_consts, 1)
            pool.iota(tile_index[:], [[1, TILES], [0, E]], base=0, channel_multiplier=0,
                      allow_small_or_imprecise_dtypes=True).then_inc(more_consts, 1)
            pool.iota(tile_row[:], [[P, TILES]], base=E * N, channel_multiplier=0,
                      allow_small_or_imprecise_dtypes=True).then_inc(more_consts, 1)
            pool.iota(token_rows[:, :, INDEX].rearrange("p (b j) -> p b j", j=QT), [[S, B], [1, QT]], base=0,
                      channel_multiplier=QT, allow_small_or_imprecise_dtypes=True).then_inc(more_consts, 1)
            pool.memset(seen[:], 0.0).then_inc(more_consts, 1)
            pool.wait_ge(more_consts, 1)
            pool.affine_select(out=before[:], in_=ones_bf[:], compare_op=ALU.is_gt, fill=0.0, base=0,
                               pattern=[[1, P]], channel_multiplier=-1).then_inc(more_consts, 1)
            pool.affine_select(out=upto[:], in_=ones[0:1, 0:E * E].rearrange("p (e k) -> p e k", k=E), compare_op=ALU.is_ge,
                               fill=0.0, base=0, pattern=[[1, E], [-1, E]], channel_multiplier=0).then_inc(more_consts, 1)

            def second_deviation(k):
                n = len(ROUTED[k])
                pool.wait_ge(var2_ready, k + 1)
                pool.tensor_tensor(rstd2[:, 0:n], var_eps2[:, 0:n], minus_half[:, 0:n], ALU.pow).then_inc(rstd2_ready, 1)

            def scatter_rows(k):
                if k == 0:
                    pool.wait_ge(regions_cleared, 32)
                pool.wait_ge(rows_ready, k + 1)
                for t in ROUTED[k]:
                    pool.indirect_dma_start(out=regions, out_offset=bass.IndirectOffsetOnAxis(ap=row_of[:, t:t + 1], axis=0),
                                            in_=token_rows[:, t, :], in_offset=None).then_inc(
                                                scattered_early if k < EARLY_BATCHES else scattered, 16)

            def attention(W, signals):
                HB = heads_a_bank(W)
                for j in range(QT):
                    hidden_keys = mask_u8[:, j, SK - W:SK].unsqueeze(1).to_broadcast([P, HB, W])
                    last = pool.tensor_scalar(mask_bias[:, j, :].rearrange("p (h w) -> p h w", w=W),
                                              hidden_keys, MASKED, None, ALU.mult)
                last.then_inc(signals["mask_ready"], 1)
                pool.wait_ge(x_loaded[0], 16)
                pool.wait_ge(x_loaded[1], 16)
                pool.wait_ge(bo_loaded, 16)
                pool.tensor_tensor(x_bo[:], x_tok[:].rearrange("p b j d -> p (b j) d"), bo_wide[:].to_broadcast([P, NT, D]),
                                   ALU.add).then_inc(x_bo_ready, 1)
                for kind, at, *rest in steps(W):
                    if kind == "inverse":
                        n, r = number(W, *at), rest[0]
                        pool.wait_ge(signals["inv_ready"], 2 * n + r + 1)
                        p = probs[:, n % 2, r, :].rearrange("p (h w) -> p h w", w=W)
                        inv = inv_sum[:, n % 2, r, 0:HB].unsqueeze(2).to_broadcast([P, HB, W])
                        pool.tensor_tensor(p, p, inv, ALU.mult).then_inc(signals["normalised"], 1)
                    elif kind == "ln2":
                        second_deviation(at)
                    elif kind == "scatter":
                        scatter_rows(at)

            pool.wait_ge(flag_ready, 1)
            flag = pool.value_load(short_flag[0:1, 0:1], min_val=0, max_val=1)
            with pool.If(flag == 1):
                attention(TAIL, short)
            with pool.Else():
                attention(SK, full)

            def scatter_result(i):
                pool.wait_ge(tile_loaded[i], 16)
                pool.tensor_copy(token_of[:, i:i + 1], rows_at(i, slice(INDEX, INDEX + 1))).then_inc(tokens_ready, 1)
                pool.wait_ge(tokens_ready, i + 1)
                pool.wait_ge(result_ready, i + 1)
                pool.indirect_dma_start(out=out_rows, out_offset=bass.IndirectOffsetOnAxis(ap=token_of[:, i:i + 1], axis=0),
                                        in_=results_at(i), in_offset=None, bounds_check=N - 1,
                                        oob_is_err=False).then_inc(result_scattered, 16)

            def scatter_from(i):
                if i == ALL:
                    pool.wait_ge(result_scattered, 16 * ALL)
                    return
                with pool.If(used > i):
                    scatter_result(i)
                    scatter_from(i + 1)
                with pool.Else():
                    pool.wait_ge(result_scattered, 16 * i)

            for i in range(EARLY):
                scatter_result(i)
            pool.wait_ge(table_ready, 1)
            used = pool.value_load(used_tiles[0:1, 0:1], min_val=NT, max_val=ALL)
            for i in range(EARLY, NT):
                scatter_result(i)
            scatter_from(NT)

        @block.scalar
        def _(act):
            act.dma_start(wq_sb[:], Wq).then_inc(wq_loaded, 16)
            act.dma_start(bias_rows[0:FT, :], bq.rearrange("(m p) -> m p", p=P)).then_inc(biases_loaded, 16)
            act.dma_start(bias_rows[FT:2 * FT, :], bk.rearrange("(m p) -> m p", p=P)).then_inc(biases_loaded, 16)
            act.dma_start(bias_rows[2 * FT:3 * FT, :], bv.rearrange("(m p) -> m p", p=P)).then_inc(biases_loaded, 16)
            act.dma_start(bias_rows[3 * FT:NB, :], b1.rearrange("e (c p) -> (e c) p", p=P)).then_inc(biases_loaded, 16)
            act.dma_start(bo_wide[:], bo.partition_broadcast(P).unsqueeze(1)).then_inc(bo_loaded, 16)

            for i in range(2):
                act.wait_ge(x_filled, i + 1)
                act.activation(normed_T[:, i * BANK:(i + 1) * BANK], x_bank[i][:], ACT.Copy).then_inc(x_drained, 1)

            def gate_sums(k):
                act.wait_ge(gate_max_ready, k + 1)
                for j in range(len(ROUTED[k])):
                    last = act.activation(exps[:, j, :], logits[:, j, :], ACT.Exp, bias=gate_neg_max[:, j:j + 1],
                                          accum_out=gate_sum[:, j:j + 1])
                last.then_inc(gate_sum_ready, 1)

            def turned_rows(i):
                act.wait_ge(turned, i + 1)
                act.activation(rows_T_at(i), banks[4 + i % 2][:, 0:P], ACT.Copy).then_inc(turn_drained, 1)

            def relu(i):
                act.wait_ge(hid_filled, i + 1)
                if i >= 2:
                    act.wait_ge(y_filled, i - 1)
                for c in range(HC):
                    act.activation(hidden[:, i % 2, c * P:(c + 1) * P], banks[i % 2][:, c * P:(c + 1) * P], ACT.Relu,
                                   bias=b1_stage[:, i % 3, c:c + 1]).then_inc(relu_done, 1)

            def relu_tile(i):
                if i + 1 < ALL:
                    turned_rows(i + 1)
                relu(i)

            def stage_early(i):
                act.wait_ge(early_table_ready, 1)
                act.wait_ge(experts_loaded, 48)
                act.wait_ge(x1_ready, NT)
                e = act.value_load(expert_of[0:1, i:i + 1], min_val=0, max_val=E - 1)
                act.activation(b1_stage[:, i, :].unsqueeze(1),
                               bias_T[:, 3 * FT:NB].rearrange("p (e c) -> p e c", c=HC)[:, bass.ds(e, 1), :], ACT.Copy)
                act.activation(b2_early[:, i, :].unsqueeze(1), b2_wide[:, bass.ds(e, 1), :], ACT.Copy)
                act.activation(w1_stage[:, i, :].unsqueeze(1), w1_sb[:, bass.ds(e, 1), :], ACT.Copy).then_inc(early_staged, 1)

            def attention(W, signals):
                HB = heads_a_bank(W)
                width = SK if W == SK else B * W

                def exponentials(n, r):
                    act.wait_ge(signals["max_ready"], 2 * n + r + 1)
                    if n >= 2:
                        act.wait_ge(signals["turn_filled"], 2 * (n - 2) + r + 1)
                    for i in range(HB):
                        c = slice(i * W, (i + 1) * W)
                        last = act.activation(probs[:, n % 2, r, c], score_bank[n % 2][r][:, c], ACT.Exp,
                                              bias=neg_max[:, n % 2, r, i:i + 1],
                                              accum_out=row_sum[:, n % 2, r, i:i + 1])
                    last.then_inc(signals["exp_done"], 1)

                def odd_heads(stage, bank, count):
                    act.wait_ge(signals["filled"], count)
                    act.wait_ge(zeros_ready, 3)
                    col = (FT if stage[0] == "k" else 2 * FT) + stage[1]
                    for i in range(BANK // width):
                        if W == SK:
                            to, from_ = kv_full[DH:P, stage[1], 1, :], bank[DH:P, :]
                        else:
                            to = (k_short if stage[0] == "k" else v_short)[DH:P, stage[1] + i, :, 1, :]
                            from_ = bank[DH:P, i * width:(i + 1) * width].rearrange("p (b k) -> p b k", b=B)
                        last = act.activation(to, from_, ACT.Identity, bias=bias_T[DH:P, col + i:col + i + 1])
                    last.then_inc(signals["odd_drained"], 1)

                count = turns = 0
                for kind, at, *rest in steps(W):
                    if kind == "work":
                        count += 1
                        if odd_on_scalar(at):
                            odd_heads(at, rest[0], count)
                    elif kind == "exp":
                        exponentials(number(W, *at), rest[0])
                    elif kind == "wide_exp":
                        n = number(W, *at)
                        act.wait_ge(signals["centered"], 1)
                        act.activation(probs[:, n % 2, 1, :], probs[:, n % 2, 1, :], ACT.Exp).then_inc(signals["exp_done"], 1)
                    elif kind == "turn":
                        turns += 1
                    elif kind == "last_turn":
                        turns += 1
                        act.wait_ge(signals["turn_filled"], turns)
                        act.activation(probs_T[:, rest[0], :], turn_bank[rest[0]][:], ACT.Copy).then_inc(signals["turn_drained"], 1)
                    elif kind == "logits":
                        gate_sums(at)
                    elif kind == "early_turn":
                        turned_rows(at)
                    elif kind == "early_stage":
                        stage_early(at)
                    elif kind == "early_hidden":
                        relu(at)

            act.wait_ge(flag_ready, 1)
            flag = act.value_load(short_flag[0:1, 0:1], min_val=0, max_val=1)
            with act.If(flag == 1):
                attention(TAIL, short)
            with act.Else():
                attention(SK, full)

            stage_early(2)
            turned_rows(2)
            relu(1)
            relu(2)
            turned_rows(EARLY)
            act.wait_ge(table_ready, 1)
            used = act.value_load(used_tiles[0:1, 0:1], min_val=NT, max_val=ALL)
            for i in range(EARLY, NT):
                relu_tile(i)
            for i in range(NT, ALL):
                with act.If(used > i):
                    relu_tile(i)

        @block.tensor
        def _(pe):
            def queries(bank, b, m0):
                for m in range(m0, m0 + 2):
                    last = pe.matmul(bank[:, (m - m0) * S:(m - m0 + 1) * S], wq_sb[:, m * P:(m + 1) * P],
                                     normed_T[:, b * S:(b + 1) * S], start=True, stop=True)
                return last

            def warm_up(bank, products):
                for _ in range(products):
                    last = pe.matmul(bank[:, 0:P], ones[:], ones[:], start=True, stop=True)
                return last

            pe.wait_ge(consts_made, 3)
            warm_up(banks[0], 12)
            pe.wait_ge(normed_ready, 1)
            for t in range(4):
                last = pe.transpose(x_bank[0][:, t * P:(t + 1) * P], normed[:, t, :], ident[:])
            last.then_inc(x_filled, 1)
            pe.wait_ge(biases_loaded, 64)
            pe.transpose(work_bank[:, 0:NB], bias_rows[:], ident[0:NB, 0:NB]).then_inc(bias_filled, 1)
            pe.wait_ge(tail_loaded, 32)
            for t in range(2):
                last = pe.transpose(tail_bank[:, t * P:(t + 1) * P], ctx_tail[:, t, :], ident[:])
            last.then_inc(tail_filled, 1)
            pe.wait_ge(wq_loaded, 16)
            pe.wait_ge(x_drained, 1)
            queries(q0_bank[0], 0, 0).then_inc(q0_filled, 1)
            pe.wait_ge(far_min_ready, 1)
            pe.matmul(out_bank[0:1, 0:1], far_min[:], ones[:, 0:1], start=True, stop=True).then_inc(flag_filled, 1)
            queries(q0_bank[1], 0, 2).then_inc(q0_filled, 1)
            pe.wait_ge(normed_ready, 2)
            for t in range(4):
                last = pe.transpose(x_bank[1][:, t * P:(t + 1) * P], normed[:, 4 + t, :], ident[:])
            last.then_inc(x_filled, 1)
            for i in range(2, FT // 2 - 1):
                queries(q0_bank[i], 0, 2 * i).then_inc(q0_filled, 1)
            pe.wait_ge(x_drained, 2)
            pe.wait_ge(bias_ready, 1)
            pe.wait_ge(tail_drained, 1)

            def transpose_rows(k):
                pe.wait_ge(h_ready, k + 1)
                for j in range(len(ROUTED[k])):
                    last = pe.transpose(normed2_bank(k)[:, j * P:(j + 1) * P], normed2[:, j, :], ident[:])
                last.then_inc(normed2_filled, 1)

            def gate_logits(k):
                if k == 0:
                    pe.wait_ge(router_loaded, 32)
                pe.wait_ge(normed2_drained, k + 1)
                for j in range(len(ROUTED[k])):
                    last = pe.matmul(work_bank[:, j * E:(j + 1) * E], normed2_T[:, j * P:(j + 1) * P], wg_sb[:],
                                     start=True, stop=True)
                last.then_inc(logits_filled, 1)

            def expert_ranks(k):
                if k == 0:
                    pe.wait_ge(more_consts, 13)
                pe.wait_ge(onehot_ready, k + 1)
                if k:
                    pe.wait_ge(seen_ready, k)
                for j in range(len(ROUTED[k])):
                    ranked = ranks_bank(k)[:, j * E:(j + 1) * E]
                    pe.matmul(ranked, before[:], onehot[:, j, :], start=True, stop=False)
                    for i in range(j):
                        pe.matmul(ranked, ones_bf[:], onehot[:, i, :], start=False, stop=False)
                    last = pe.matmul(ranked, ones_bf[:], seen[:], start=False, stop=True)
                last.then_inc(ranks_filled, 1)

            def turn_rows(i):
                if i >= 2:
                    pe.wait_ge(turn_drained, i - 1)
                pe.wait_ge(slot_ready, i + 1)
                pe.transpose(banks[4 + i % 2][:, 0:P], slot_normed_at(i), ident[:]).then_inc(turned, 1)

            def hidden_tile(i):
                if EARLY <= i < ALL - 1:
                    turn_rows(i + 1)
                pe.wait_ge(turn_drained, i + 1)
                if i < EARLY:
                    pe.wait_ge(early_staged, i + 1)
                else:
                    pe.wait_ge(staged, i - EARLY + 1)
                if i >= 2:
                    pe.wait_ge(relu_done, HC * (i - 1))
                for c in range(HC):
                    last = pe.matmul(banks[i % 2][:, c * P:(c + 1) * P], w1_stage[:, i % 3, c * P:(c + 1) * P],
                                     rows_T_at(i), start=True, stop=True)
                last.then_inc(hid_filled, 1)

            def result_tile(i):
                e = pe.value_load(expert_of[0:1, i:i + 1], min_val=0, max_val=E - 1)
                if i >= 2:
                    pe.wait_ge(plus_ready, i - 1)
                if i == 1:
                    pe.wait_ge(ranks_drained, B + 1)
                for c in range(HC):
                    pe.wait_ge(relu_done, HC * i + c + 1)
                    last = pe.matmul(banks[2 + i % 2][:, 0:D].unsqueeze(1), hidden[:, i % 2, c * P:(c + 1) * P],
                                     w2_sb[:, bass.ds(e, 1), c * D:(c + 1) * D], start=(c == 0), stop=(c == HC - 1))
                last.then_inc(y_filled, 1)

            def attention(W, signals):
                HB = heads_a_bank(W)
                width = SK if W == SK else B * W
                count = turns = odd = 0
                free_when = {}
                count_at = {}

                def claim(bank, *reads):
                    for signal, value in free_when.get(id(bank), ()):
                        pe.wait_ge(signal, value)
                    free_when[id(bank)] = reads

                def work(stage, bank):
                    nonlocal count, odd
                    count += 1
                    count_at[stage] = count
                    kv = stage[0] in ("k", "v")
                    odd += odd_on_scalar(stage)
                    claim(bank, (signals["drained"], count), *([(signals["odd_drained"], odd)] if odd_on_scalar(stage) else []))
                    if stage[0] == "ctx":
                        pe.wait_ge(signals["ctx_loaded"], 16 * (stage[1] + 1))
                        for t in range(SK // P):
                            last = pe.transpose(bank[:, t * P:(t + 1) * P], ctx_all[:, t, :], ident[:])
                    elif kv:
                        weights = wk_sb if stage[0] == "k" else wv_sb
                        if stage[1] == 0:
                            pe.wait_ge(wk_loaded if stage[0] == "k" else wv_loaded, 16)
                            if W == SK:
                                pe.wait_ge(signals["drained"], max(n for s, n in count_at.items() if s[0] == "ctx"))
                        for i in range(BANK // width):
                            m = stage[1] + i
                            last = pe.matmul(bank[:, i * width:(i + 1) * width], weights[:, m * P:(m + 1) * P],
                                             ctx_T[:, 0:width], start=True, stop=True)
                    elif stage[0] == "q":
                        last = queries(bank, *stage[1:])
                    else:
                        _, b, c = stage
                        if c == 0:
                            pe.wait_ge(signals["drained"], max(n for s, n in count_at.items() if s[0] == "v"))
                            pe.wait_ge(signals["odd_drained"], odd)
                            if b == 0:
                                pe.wait_ge(wo_loaded, 16)
                        for k in range(4):
                            blk = c * 4 + k
                            if W == SK:
                                h, t = blk // (SK // P), blk % (SK // P)
                                m, values = h // 2, kv_full[:, h // 2, h % 2, t * P:(t + 1) * P]
                            else:
                                m, values = blk, v_short[:, blk, b, :, :].rearrange("p r k -> p (r k)")
                            last = pe.matmul(bank[:, k * D:(k + 1) * D], values, wo_sb[:, m, :], start=True, stop=True)
                    last.then_inc(signals["filled"], 1)

                def score(b, j, g):
                    n = number(W, b, j, g)
                    if n == 0:
                        pe.wait_ge(consts_made, 4)
                        pe.wait_ge(signals["mask_ready"], 1)
                    if g == 0 and j == 0:
                        if b == 0:
                            pe.wait_ge(q0_drained, FT // 2 - 1)
                        pe.wait_ge(signals["drained"], max(n for s, n in count_at.items() if s[0] == "k" or s[:2] == ("q", b)))
                        pe.wait_ge(signals["odd_drained"], odd)
                    for r in range(2):
                        bank = score_bank[n % 2][r]
                        if n >= 2:
                            pe.wait_ge(signals["exp_done"], 2 * (n - 2) + r + 1)
                        pe.matmul(bank[:], ident_bf[:], mask_bias[:, j, :], start=True, stop=False, skip_group_check=True)
                        if W == SK:
                            h = 2 * g + r
                            last = pe.matmul(bank[:], q_T[:, b % 2, h // 2, j * P:(j + 1) * P], kv_full[:, h // 2, h % 2, :],
                                             start=False, stop=True, skip_group_check=True)
                        else:
                            for i in range(HB // 2):
                                m = r * HB // 2 + i
                                last = pe.matmul(bank[:, i * 2 * W:(i + 1) * 2 * W], q_T[:, b % 2, m, j * P:(j + 1) * P],
                                                 k_short[:, m, b, :, :].rearrange("p r k -> p (r k)"),
                                                 start=False, stop=i == HB // 2 - 1, skip_group_check=True)
                        last.then_inc(signals["scored"], 1)

                def turn(b, j, g, r):
                    nonlocal turns
                    n = number(W, b, j, g)
                    turns += 1
                    claim(turn_bank[r], (signals["turn_drained"], turns))
                    if W != SK and (b, j, r) == (B - 1, QT - 1, 1):
                        pe.wait_ge(signals["wide_normalised"], 1)
                    else:
                        pe.wait_ge(signals["normalised"], 2 * n + r + 1)
                    for k in range(4):
                        last = pe.transpose(turn_bank[r][:, k * P:(k + 1) * P], probs[:, n % 2, r, k * P:(k + 1) * P], ident[:])
                    last.then_inc(signals["turn_filled"], 1)

                def output(b, j, g, r):
                    if g == 0 and r == 0:
                        if b or j:
                            pe.wait_ge(x1_ready, b * QT + j)
                        if j == 0:
                            pe.wait_ge(signals["drained"], count_at["vo", b, 2 * groups(W) - 1])
                    base = 0 if W == SK else (b % 2) * 8
                    pe.wait_ge(signals["turn_drained"], turns - 1 + r)
                    for k in range(4):
                        first = g == 0 and r == 0 and k == 0
                        final = g == groups(W) - 1 and r == 1 and k == 3
                        last = pe.matmul(out_bank[:, 0:D], probs_T[:, r, k * P:(k + 1) * P],
                                         vo[:, base + (g * 2 + r) * 4 + k, :], start=first, stop=final)
                    last.then_inc(signals["out_filled"], 1)

                for kind, at, *rest in steps(W):
                    if kind == "work":
                        work(at, rest[0])
                    elif kind == "score":
                        score(*at)
                    elif kind in ("turn", "last_turn"):
                        turn(*at, rest[0])
                    elif kind == "warm_up":
                        warm_up(rest[0], at)
                    elif kind == "early_counts":
                        claim(work_bank, (early_counts_ready, 1))
                        pe.wait_ge(onehot_ready, EARLY_BATCHES)
                        pe.wait_ge(seen_ready, EARLY_BATCHES - 1)
                        for i in range(QT):
                            pe.matmul(work_bank[0:1, 0:E], ones_bf[:, 0:1], onehot[:, i, :], start=(i == 0), stop=False)
                        pe.matmul(work_bank[0:1, 0:E], ones_bf[:, 0:1], seen[:], start=False,
                                  stop=True).then_inc(early_counts_filled, 1)
                    elif kind == "early_turn":
                        turn_rows(at)
                    elif kind == "early_hidden":
                        hidden_tile(at)
                    elif kind == "out":
                        output(*at, rest[0])
                    elif kind == "h_T":
                        claim(normed2_bank(at), (normed2_drained, at + 1))
                        transpose_rows(at)
                    elif kind == "logits":
                        claim(work_bank, (logits_drained, at + 1))
                        gate_logits(at)
                    elif kind == "rank":
                        claim(ranks_bank(at), (ranks_drained, at + 1))
                        expert_ranks(at)

            pe.wait_ge(flag_ready, 1)
            flag = pe.value_load(short_flag[0:1, 0:1], min_val=0, max_val=1)
            with pe.If(flag == 1):
                attention(TAIL, short)
            with pe.Else():
                attention(SK, full)
            pe.wait_ge(logits_drained, B + 1)
            pe.matmul(work_bank[0:1, 0:E], ones_bf[:, 0:1], seen[:], start=True, stop=False)
            pe.matmul(work_bank[0:1, 0:E], ones_bf[:, 0:1], onehot[:, 0, :], start=False, stop=True).then_inc(counts_filled, 1)
            result_tile(0)
            turn_rows(2)
            hidden_tile(1)
            hidden_tile(2)
            result_tile(1)
            result_tile(2)
            pe.wait_ge(x1_ready, NT)
            warm_up(out_bank, 6)

            def from_tile(i):
                if i == ALL:
                    result_tile(i - 1)
                    return
                with pe.If(used > i):
                    hidden_tile(i)
                    result_tile(i - 1)
                    from_tile(i + 1)
                with pe.Else():
                    result_tile(i - 1)

            pe.wait_ge(table_ready, 1)
            used = pe.value_load(used_tiles[0:1, 0:1], min_val=NT, max_val=ALL)
            turn_rows(EARLY)
            hidden_tile(EARLY)
            for i in range(EARLY + 1, NT):
                hidden_tile(i)
                result_tile(i - 1)
            from_tile(NT)

        @block.vector
        def _(dve):
            def chained(signal):
                links = 0

                def after(instruction):
                    nonlocal links
                    links += 1
                    instruction.then_inc(signal, 1)
                    dve.wait_ge(signal, links)
                return after

            after = chained(dve_done)

            dve.memset(zero_padded[:, FT * SK:FT * SK + DVE_ZEROS], 0.0).then_inc(zeros_ready, 1)
            x_flat = x_tok[:].rearrange("p b j d -> p (b j) d")
            def statistics_half(i):
                tiles = range(i * NT // 2, (i + 1) * NT // 2)
                dve.wait_ge(x_loaded[i], 16)
                for t in tiles:
                    last = dve.bn_stats(stats[:, t, :], x_flat[:, t, :])
                after(last)
                for t in tiles:
                    last = dve.bn_aggr(mean_var[:, t, :], stats[:, t, :])
                after(last)
                c = slice(tiles[0], tiles[-1] + 1)
                dve.tensor_scalar(var_eps[:, c], mean_var[:, c, 1], EPS, None, ALU.add).then_inc(var_ready, 1)

            def normalise_half(i):
                dve.wait_ge(rstd_ready, i + 1)
                for t in range(i * NT // 2, (i + 1) * NT // 2):
                    last = dve.tensor_scalar(normed[:, t, :], x_flat[:, t, :], mean_var[:, t, 0:1], rstd[:, t:t + 1],
                                             ALU.subtract, ALU.mult)
                last.then_inc(normed_ready, 1)

            statistics_half(0)
            normalise_half(0)
            statistics_half(1)
            dve.wait_ge(mask_loaded, 16)
            dve.tensor_reduce(far_min[:], mask_u8[:, :, 0:SK - TAIL], AX.XY, ALU.min).then_inc(far_min_ready, 1)
            dve.wait_ge(bias_filled, 1)
            dve.tensor_copy(bias_T[:], work_bank[:, 0:NB]).then_inc(bias_ready, 1)
            normalise_half(1)
            dve.wait_ge(bias_ready, 1)
            dve.tensor_scalar(bq_scaled[:], bias_T[:, 0:FT], SCALE, None, ALU.mult).then_inc(bias_ready, 1)
            dve.wait_ge(tail_filled, 1)
            dve.tensor_copy(ctx_T[:, 0:B * TAIL], tail_bank[:, 0:B * TAIL]).then_inc(tail_drained, 1)
            dve.wait_ge(flag_filled, 1)
            dve.tensor_scalar(short_flag[:], out_bank[0:1, 0:1], float(P), None, ALU.is_equal).then_inc(flag_ready, 1)

            after(dve.tensor_reduce(row_min[:], mask_u8[:], AX.X, ALU.min))
            after(dve.tensor_scalar(blown[:], row_min[:], HUGE, HUGE, ALU.mult, ALU.mult))
            after(dve.tensor_tensor(dead_row[:], blown[:], blown[:], ALU.subtract))

            def drain_queries(bank, b, m):
                bias = bq_scaled[:, m:m + 2].unsqueeze(2).to_broadcast([P, 2, S])
                return dve.scalar_tensor_tensor(out=q_T[:, b % 2, m:m + 2, :], in0=bank[:].rearrange("p (m s) -> p m s", s=S),
                                                scalar=SCALE, in1=bias, op0=ALU.mult, op1=ALU.add)

            dve.wait_ge(bias_ready, 2)
            for i in range(FT // 2 - 1):
                dve.wait_ge(q0_filled, i + 1)
                drain_queries(q0_bank[i], 0, 2 * i).then_inc(q0_drained, 1)

            def second_statistics(k, after):
                for j, t in enumerate(ROUTED[k]):
                    dve.wait_ge(x1_ready, t + 1)
                    last = dve.bn_stats(stats2[:, j, :], token_rows[:, t, 0:D])
                after(last)
                for j in range(len(ROUTED[k])):
                    last = dve.bn_aggr(mean_var2[:, j, :], stats2[:, j, :])
                after(last)
                n = len(ROUTED[k])
                dve.tensor_scalar(var_eps2[:, 0:n], mean_var2[:, 0:n, 1], EPS, None, ALU.add).then_inc(var2_ready, 1)

            def second_normalise(k):
                dve.wait_ge(rstd2_ready, k + 1)
                if k:
                    dve.wait_ge(normed2_filled, k)
                for j, t in enumerate(ROUTED[k]):
                    last = dve.tensor_scalar(normed2[:, j, :], token_rows[:, t, 0:D], mean_var2[:, j, 0:1],
                                             rstd2[:, j:j + 1], ALU.subtract, ALU.mult)
                last.then_inc(h_ready, 1)
                t, n = ROUTED[k][0], len(ROUTED[k])
                dve.tensor_copy(token_rows[:, t:t + n, MEAN], mean_var2[:, 0:n, 0])
                dve.tensor_copy(token_rows[:, t:t + n, RSTD], rstd2[:, 0:n])

            def drain_normed(k):
                n = len(ROUTED[k])
                dve.wait_ge(normed2_filled, k + 1)
                dve.tensor_copy(normed2_T[:, 0:n * P], normed2_bank(k)[:, 0:n * P]).then_inc(normed2_drained, 1)

            def wide(column, n):
                return column[:, 0:n].unsqueeze(2).to_broadcast([P, n, E])

            def choose(k, after):
                n = len(ROUTED[k])
                if k == 0:
                    dve.wait_ge(more_consts, 13)
                    dve.wait_ge(router_loaded, 32)
                dve.wait_ge(logits_filled, k + 1)
                dve.tensor_tensor(logits[:, 0:n, :], work_bank[:, 0:n * E].rearrange("p (j e) -> p j e", e=E),
                                  bg_wide[:].to_broadcast([P, n, E]), ALU.add).then_inc(logits_drained, 1)
                dve.wait_ge(logits_drained, k + 1)
                after(dve.tensor_reduce(gate_max[:, 0:n], logits[:, 0:n, :], AX.X, ALU.max))
                for j in range(n):
                    last = dve.scalar_tensor_tensor(out=candidates[:, j, :], in0=logits[:, j, :], scalar=gate_max[:, j:j + 1],
                                                    in1=falling[:, j, :], op0=ALU.is_equal, op1=ALU.mult)
                after(last)
                after(dve.tensor_reduce(chosen[:, 0:n], candidates[:, 0:n, :], AX.X, ALU.max))
                dve.tensor_tensor(onehot[:, 0:n, :], falling[:, 0:n, :], wide(chosen, n), ALU.is_equal).then_inc(onehot_ready, 1)
                dve.tensor_scalar(gate_neg_max[:, 0:n], gate_max[:, 0:n], -1.0, None, ALU.mult).then_inc(gate_max_ready, 1)

            def place(k, after):
                t, n = ROUTED[k][0], len(ROUTED[k])
                dve.wait_ge(ranks_filled, k + 1)
                dve.tensor_tensor(ranks[:, 0:n, :], ranks_bank(k)[:, 0:n * E].rearrange("p (j e) -> p j e", e=E),
                                  onehot[:, 0:n, :], ALU.mult).then_inc(ranks_drained, 1)
                dve.wait_ge(ranks_drained, k + 1)
                after(dve.tensor_reduce(rank[:, 0:n], ranks[:, 0:n, :], AX.X, ALU.add))
                dve.scalar_tensor_tensor(out=row_of[:, t:t + n], in0=chosen[:, 0:n], scalar=float(N), in1=rank[:, 0:n],
                                         op0=ALU.mult, op1=ALU.add)
                dve.wait_ge(gate_sum_ready, k + 1)
                dve.reciprocal(token_rows[:, t:t + n, PROB], gate_sum[:, 0:n]).then_inc(rows_ready, 1)
                if k == len(ROUTED) - 1:
                    return
                for j in range(n - 1):
                    after(dve.tensor_tensor(seen[:], seen[:], onehot[:, j, :], ALU.add))
                dve.tensor_tensor(seen[:], seen[:], onehot[:, n - 1, :], ALU.add).then_inc(seen_ready, 1)

            def normalise_slots(i):
                dve.wait_ge(tile_loaded[i], 16)
                dve.tensor_scalar(slot_normed_at(i), rows_at(i, slice(0, D)), rows_at(i, slice(MEAN, MEAN + 1)),
                                  rows_at(i, slice(RSTD, RSTD + 1)), ALU.subtract, ALU.mult).then_inc(slot_ready, 1)

            def tile_table(tiles, count, end, row_step, row, after):
                shape = [1, count, E]
                after(dve.tensor_tensor(passed[:, 0:count, :], tile_index[:, 0:count, :],
                                        end.unsqueeze(1).to_broadcast(shape), ALU.is_ge))
                after(dve.tensor_tensor(passed_rows[:, 0:count, :], passed[:, 0:count, :],
                                        row_step.unsqueeze(1).to_broadcast(shape), ALU.mult))
                after(dve.tensor_reduce(row_f[:, 0:count], passed_rows[:, 0:count, :], AX.X, ALU.add))
                after(dve.tensor_reduce(expert_f[:, 0:count], passed[:, 0:count, :], AX.X, ALU.add))
                dve.tensor_tensor(first_row[:, tiles], row_f[:, 0:count], row, ALU.add)
                return dve.tensor_scalar(expert_of[:, tiles], expert_f[:, 0:count], float(E - 1), None, ALU.min)

            def sum_pairs(out, of, after):
                after(dve.tensor_tensor(pairs[:], of.unsqueeze(1).to_broadcast([1, E, E]), upto[:], ALU.mult))
                after(dve.tensor_reduce(out, pairs[:], AX.X, ALU.add))

            def early_table(after):
                dve.wait_ge(early_counts_ready, 1)
                after(dve.tensor_tensor(pairs[:], early_counts[:].unsqueeze(2).to_broadcast([1, E, E]), full_at[:],
                                              ALU.is_ge))
                after(dve.tensor_reduce(full_of[:], pairs[:], AX.X, ALU.add))
                sum_pairs(end_full[:], full_of[:], after)
                after(dve.tensor_scalar(end_early[:, 1:1 + E], end_full[:], float(EARLY), None, ALU.min))
                after(dve.tensor_tensor(early_of[:, 0:E], end_early[:, 1:1 + E], end_early[:, 0:E], ALU.subtract))
                dve.tensor_tensor(early_step[:], early_of[:, 1:E + 1], early_of[:, 0:E], ALU.subtract)
                after(dve.tensor_scalar(early_row_step[:], early_of[:, 0:E], -float(P), -float(N), ALU.mult, ALU.add))
                tile_table(slice(0, EARLY), EARLY, end_early[:, 1:1 + E], early_row_step[:], tile_row[:, 0:EARLY],
                           after).then_inc(early_table_ready, 1)

            def late_constants():
                dve.scalar_tensor_tensor(out=late_thresholds[:], in0=early_of[:, 0:E].unsqueeze(2).to_broadcast([1, E, E]),
                                         scalar=float(P), in1=thresholds[:], op0=ALU.mult, op1=ALU.add)
                dve.tensor_scalar(late_row_base[:], early_step[:], float(P), -float(N), ALU.mult, ALU.add)
                return dve.scalar_tensor_tensor(out=late_tile_row[:], in0=early_of[:, 0:1].to_broadcast([1, TILES]),
                                                scalar=float(P), in1=tile_row[:], op0=ALU.mult, op1=ALU.add)

            def attention(W, signals):
                HB = heads_a_bank(W)
                width = SK if W == SK else B * W
                count = 0
                after = chained(signals["dve_done"])

                def work(stage, bank):
                    nonlocal count
                    count += 1
                    dve.wait_ge(signals["filled"], count)
                    if stage[0] == "ctx":
                        last = dve.tensor_copy(ctx_T[:, 0:width], bank[:, 0:width])
                    elif stage[0] in ("k", "v"):
                        if stage[1] == 0:
                            dve.wait_ge(zeros_ready, 3)
                        many = BANK // width
                        col = (FT if stage[0] == "k" else 2 * FT) + stage[1]
                        for r in range(1 if odd_on_scalar(stage) else 2):
                            rows = slice(r * DH, (r + 1) * DH)
                            bias = bias_T[rows, col:col + many].unsqueeze(2)
                            if W == SK:
                                to = kv_full[rows, stage[1]:stage[1] + 1, r, :]
                                from_ = bank[rows, :].rearrange("p (m s) -> p m s", s=width)
                                bias = bias.to_broadcast([DH, many, width])
                            else:
                                to = (k_short if stage[0] == "k" else v_short)[rows, stage[1]:stage[1] + many, :, r, :]
                                from_ = bank[rows, :].rearrange("p (m b k) -> p m b k", b=B, k=W)
                                bias = bias.unsqueeze(3).to_broadcast([DH, many, B, W])
                            last = dve.tensor_tensor(to, from_, bias, ALU.add)
                    elif stage[0] == "q":
                        last = drain_queries(bank, *stage[1:])
                    else:
                        _, b, c = stage
                        base = (0 if W == SK else (b % 2) * 8) + c * 4
                        last = dve.tensor_copy(vo[:, base:base + 4, :], bank[:].rearrange("p (k d) -> p k d", d=D))
                    last.then_inc(signals["drained"], 1)

                turns = 0
                for kind, at, *rest in steps(W):
                    if kind == "work":
                        work(at, rest[0])
                    elif kind == "score":
                        n = number(W, *at)
                        for r in range(2):
                            dve.wait_ge(signals["scored"], 2 * n + r + 1)
                            dve.tensor_reduce(neg_max[:, n % 2, r, 0:HB],
                                              score_bank[n % 2][r][:].rearrange("p (h w) -> p h w", w=W),
                                              AX.X, ALU.max, negate=True).then_inc(signals["max_ready"], 1)
                    elif kind == "turn":
                        turns += 1
                        dve.wait_ge(signals["turn_filled"], turns)
                        dve.tensor_copy(probs_T[:, rest[0], :], turn_bank[rest[0]][:]).then_inc(signals["turn_drained"], 1)
                    elif kind == "center":
                        n = number(W, *at)
                        dve.wait_ge(signals["max_ready"], 2 * n + 2)
                        dve.wait_ge(signals["turn_filled"], 2 * (n - 2) + 2)
                        dve.tensor_tensor(probs[:, n % 2, 1, :].rearrange("p (h w) -> p h w", w=W),
                                          score_bank[n % 2][1][:].rearrange("p (h w) -> p h w", w=W),
                                          neg_max[:, n % 2, 1, 0:HB].unsqueeze(2).to_broadcast([P, HB, W]),
                                          ALU.add).then_inc(signals["centered"], 1)
                    elif kind == "wide_normalise":
                        n = number(W, *at)
                        p = probs[:, n % 2, 1, :].rearrange("p (h w) -> p h w", w=W)
                        dve.wait_ge(signals["exp_done"], 2 * n + 2)
                        after(dve.tensor_reduce(row_sum[:, n % 2, 1, 0:HB], p, AX.X, ALU.add))
                        after(dve.reciprocal(inv_sum[:, n % 2, 1, 0:HB], row_sum[:, n % 2, 1, 0:HB]))
                        dve.tensor_tensor(p, p, inv_sum[:, n % 2, 1, 0:HB].unsqueeze(2).to_broadcast([P, HB, W]),
                                          ALU.mult).then_inc(signals["wide_normalised"], 1)
                    elif kind == "inverse":
                        n, r = number(W, *at), rest[0]
                        dve.wait_ge(signals["exp_done"], 2 * n + r + 1)
                        dve.reciprocal(inv_sum[:, n % 2, r, 0:HB], row_sum[:, n % 2, r, 0:HB]).then_inc(signals["inv_ready"], 1)
                    elif kind == "out":
                        b, j, g = at
                        if g == groups(W) - 1 and rest[0] == 1:
                            if b == 0 and j == 0:
                                dve.wait_ge(x_bo_ready, 1)
                            dve.wait_ge(signals["out_filled"], 2 * number(W, *at) + 2)
                            dve.scalar_tensor_tensor(out=token_rows[:, b * QT + j, 0:D], in0=out_bank[:, 0:D],
                                                     scalar=dead_row[:, j:j + 1], in1=x_bo[:, b * QT + j, :],
                                                     op0=ALU.add, op1=ALU.add).then_inc(x1_ready, 1)
                    elif kind == "ln2":
                        second_statistics(at, after)
                    elif kind == "normalise":
                        second_normalise(at)
                    elif kind == "h_T":
                        drain_normed(at)
                    elif kind == "logits":
                        choose(at, after)
                    elif kind == "rank":
                        place(at, after)
                    elif kind == "early_counts":
                        dve.wait_ge(early_counts_filled, 1)
                        dve.tensor_copy(early_counts[:], work_bank[0:1, 0:E]).then_inc(early_counts_ready, 1)
                    elif kind == "early_table":
                        early_table(after)
                    elif kind == "late_constants":
                        late_constants()
                    elif kind == "early_slots":
                        normalise_slots(at)

            dve.wait_ge(flag_ready, 1)
            flag = dve.value_load(short_flag[0:1, 0:1], min_val=0, max_val=1)
            with dve.If(flag == 1):
                attention(TAIL, short)
            with dve.Else():
                attention(SK, full)
            dve.wait_ge(counts_filled, 1)
            after(dve.tensor_tensor(pairs[:], work_bank[0:1, 0:E].unsqueeze(2).to_broadcast([1, E, E]), late_thresholds[:],
                                    ALU.is_gt))
            after(dve.tensor_reduce(late_of[:], pairs[:], AX.X, ALU.add))
            dve.scalar_tensor_tensor(out=late_row_step[:], in0=late_of[:], scalar=-float(P), in1=late_row_base[:],
                                     op0=ALU.mult, op1=ALU.add)
            sum_pairs(end_of[:], late_of[:], after)
            dve.tensor_scalar(used_tiles[:], end_of[:, E - 1:E], float(EARLY), None, ALU.add)
            tile_table(slice(EARLY, ALL), TILES, end_of[:], late_row_step[:], late_tile_row[:], after).then_inc(table_ready, 1)

            dve.wait_ge(table_ready, 1)
            dve.wait_ge(experts_loaded, 48)

            def stage_weights(i):
                e = dve.value_load(expert_of[0:1, i:i + 1], min_val=0, max_val=E - 1)
                dve.wait_ge(relu_done, HC * (i - 2))
                dve.tensor_copy(b1_stage[:, i % 3, :].unsqueeze(1),
                                bias_T[:, 3 * FT:NB].rearrange("p (e c) -> p e c", c=HC)[:, bass.ds(e, 1), :])
                dve.tensor_copy(w1_stage[:, i % 3, :].unsqueeze(1), w1_sb[:, bass.ds(e, 1), :]).then_inc(staged, 1)
                return e

            def finish_tile(i, b2_of_expert):
                dve.wait_ge(y_filled, i + 1)
                dve.tensor_tensor(plus_b2[:, i % 2, :].unsqueeze(1), banks[2 + i % 2][:, 0:D].unsqueeze(1),
                                  b2_of_expert, ALU.add).then_inc(plus_ready, 1)
                dve.wait_ge(plus_ready, i + 1)
                dve.scalar_tensor_tensor(out=results_at(i), in0=plus_b2[:, i % 2, :], scalar=rows_at(i, slice(PROB, PROB + 1)),
                                         in1=rows_at(i, slice(0, D)), op0=ALU.mult, op1=ALU.add).then_inc(result_ready, 1)

            def prepare_after(i):
                if i + 2 < ALL:
                    normalise_slots(i + 2)
                return stage_weights(i + 1) if i + 1 < ALL else None

            def from_tile(i, before_e, e):
                if i == ALL:
                    finish_tile(i - 1, b2_wide[:, bass.ds(before_e, 1), :])
                    return
                with dve.If(used > i):
                    next_e = prepare_after(i)
                    finish_tile(i - 1, b2_wide[:, bass.ds(before_e, 1), :])
                    from_tile(i + 1, e, next_e)
                with dve.Else():
                    finish_tile(i - 1, b2_wide[:, bass.ds(before_e, 1), :])

            before_e = None
            for i in range(EARLY):
                if i == EARLY - 1:
                    e = stage_weights(EARLY)
                dve.wait_ge(early_staged, i + 1)
                finish_tile(i, b2_early[:, i:i + 1, :])
            normalise_slots(EARLY)
            normalise_slots(EARLY + 1)
            for i in range(EARLY, NT):
                next_e = prepare_after(i)
                if i > EARLY:
                    finish_tile(i - 1, b2_wide[:, bass.ds(before_e, 1), :])
                before_e, e = e, next_e
            used = dve.value_load(used_tiles[0:1, 0:1], min_val=NT, max_val=ALL)
            from_tile(NT, before_e, e)


_INS = ["x", "ctx_1024", "mask_1xSxS2_bk1", "L0_xattn_Wq", "L0_xattn_bq", "L0_xattn_Wk", "L0_xattn_bk",
        "L0_xattn_Wv", "L0_xattn_bv", "L0_xattn_Wo", "L0_xattn_bo", "L0_ffn_w_gate", "L0_ffn_b_gate",
        "L0_ffn_W1", "L0_ffn_b1", "L0_ffn_W2", "L0_ffn_b2"]


def kernel(**inputs):
    import numpy as np
    import concourse.bacc as bacc
    from concourse import mybir as _mybir
    from concourse.bass_utils import run_bass_kernel_spmd

    nc = bacc.Bacc("TRN2", target_bir_lowering=False, num_devices=1)
    arrays, args = {}, []
    for name in _INS:
        a = np.ascontiguousarray(inputs[name])
        arrays[f"in_{name}"] = a
        args.append(nc.dram_tensor(f"in_{name}", a.shape, _mybir.dt.from_np(a.dtype), kind="ExternalInput").ap())
    shape = arrays["in_x"].shape
    args.append(nc.dram_tensor("out_x", shape, _mybir.dt.float32, kind="ExternalOutput").ap())
    xattn_moe(nc, *args)
    r = run_bass_kernel_spmd(nc, [arrays], core_ids=[0])
    return np.asarray(r.results[0]["out_x"])
```
